# Optimizing a Trainium2 kernel written in Bass

```python
import numpy as np
import jax
import jax.numpy as jnp

def _softmax(x, axis=-1):
    return jax.nn.softmax(x, axis=axis)

def _gelu(x):
    return jax.nn.gelu(x, approximate=True)

def _silu(x):
    return jax.nn.silu(x)

def _sigmoid(x):
    return jax.nn.sigmoid(x)

def _layernorm(x, axis=-1, eps=1e-05):
    m = jnp.mean(x, axis=axis, keepdims=True)
    v = jnp.var(x, axis=axis, keepdims=True)
    return (x - m) / jnp.sqrt(v + eps)

def _scatter_add(tgt, idx, src, axis=0):
    return tgt.at[idx].add(src)

def _segment_sum(src, seg, n):
    return jax.ops.segment_sum(src, seg, n)
kernel_name = 'mk_recurrent_d1_jaxref_r8_101bc4'

def setup_inputs(seed: int=0):
    np.random.seed(seed)
    _w = jnp.asarray

    def _L0_attn_setup():
        import math
        import jax, jax.numpy as jnp
        import numpy as np
        B, N, D, H = (8, 128, 256, 16)
        d = D // H
        key = jax.random.key(seed)
        ks = jax.random.split(key, 4)
        scale = 1.0 / math.sqrt(D)
        x = jax.random.normal(ks[0], (B, N, D), dtype=jnp.float32)
        Wq = jax.random.normal(ks[1], (D, D), dtype=jnp.float32) * scale
        Wk = jax.random.normal(ks[2], (D, D), dtype=jnp.float32) * scale
        Wv = jax.random.normal(ks[3], (D, D), dtype=jnp.float32) * scale
        bq = jnp.zeros((D,), dtype=jnp.float32)
        bk = jnp.zeros((D,), dtype=jnp.float32)
        bv = jnp.zeros((D,), dtype=jnp.float32)
        return {'x': x, 'Wq': Wq, 'bq': bq, 'Wk': Wk, 'bk': bk, 'Wv': Wv, 'bv': bv}
    _L0_attn_in = _L0_attn_setup()

    def _L0_ffn_setup():
        import jax, jax.numpy as jnp
        import numpy as np
        E, H, I = (8, 256, 512)
        TOP_K = 1
        B, S = (1, 256)
        key = jax.random.key(seed)
        ks = jax.random.split(key, 7)
        std = 0.02
        return {'hidden_states': jax.random.normal(ks[0], (B, S, H), dtype=jnp.float32), 'router_w': jax.random.normal(ks[1], (E, H), dtype=jnp.float32) * std, 'gate_up_proj': jax.random.normal(ks[2], (E, H, 2 * I), dtype=jnp.float32) * std, 'down_proj': jax.random.normal(ks[3], (E, I, H), dtype=jnp.float32) * std, 'shared_gate_w': jax.random.normal(ks[4], (H, I), dtype=jnp.float32) * std, 'shared_up_w': jax.random.normal(ks[5], (H, I), dtype=jnp.float32) * std, 'shared_down_w': jax.random.normal(ks[6], (I, H), dtype=jnp.float32) * std}
    _L0_ffn_in = _L0_ffn_setup()
    _d = {'L0_attn_x': _L0_attn_in['x'], 'L0_attn_Wq': _L0_attn_in['Wq'], 'L0_attn_bq': _L0_attn_in['bq'], 'L0_attn_Wk': _L0_attn_in['Wk'], 'L0_attn_bk': _L0_attn_in['bk'], 'L0_attn_Wv': _L0_attn_in['Wv'], 'L0_attn_bv': _L0_attn_in['bv'], 'L0_ffn_router_w': _L0_ffn_in['router_w'], 'L0_ffn_gate_up_proj': _L0_ffn_in['gate_up_proj'], 'L0_ffn_down_proj': _L0_ffn_in['down_proj'], 'L0_ffn_shared_gate_w': _L0_ffn_in['shared_gate_w'], 'L0_ffn_shared_up_w': _L0_ffn_in['shared_up_w'], 'L0_ffn_shared_down_w': _L0_ffn_in['shared_down_w']}
    _x0 = _d['L0_attn_x']
    _d['L0_attn_x'] = jax.random.normal(jax.random.fold_in(jax.random.key(seed), 1), (16, 256, 256), dtype=_x0.dtype)
    del _x0
    return _d

def reference(L0_attn_x, L0_attn_Wq, L0_attn_bq, L0_attn_Wk, L0_attn_bk, L0_attn_Wv, L0_attn_bv, L0_ffn_router_w, L0_ffn_gate_up_proj, L0_ffn_down_proj, L0_ffn_shared_gate_w, L0_ffn_shared_up_w, L0_ffn_shared_down_w):

    def _L0_attn_ref(x, Wq, bq, Wk, bk, Wv, bv):
        import math
        import jax, jax.numpy as jnp
        import numpy as np
        B, N, D, H = (8, 128, 256, 16)
        d = D // H
        Bn, Nn, Dn = x.shape
        q = (x @ Wq + bq).reshape(Bn, Nn, H, d)
        k = (x @ Wk + bk).reshape(Bn, Nn, H, d)
        v = (x @ Wv + bv).reshape(Bn, Nn, H, d)
        scores = jnp.einsum('bnhd,bmhd->bnmh', q, k) / math.sqrt(d)
        att = jax.nn.softmax(scores, axis=2)
        attval = jnp.einsum('bnmh,bmhd->bnhd', att, v).reshape(Bn, Nn, Dn)
        return attval + x

    def _L0_ffn_ref(hidden_states, router_w, gate_up_proj, down_proj, shared_gate_w, shared_up_w, shared_down_w):
        import jax, jax.numpy as jnp
        import numpy as np
        E, H, I = (8, 256, 512)
        TOP_K = 1
        B, S = (1, 256)
        orig_shape = hidden_states.shape
        x = hidden_states.reshape(-1, H)
        T = x.shape[0]
        logits = x @ router_w.T
        top_vals, top_idx = jax.lax.top_k(logits, TOP_K)
        scores = jnp.full_like(logits, -jnp.inf)
        scores = scores.at[jnp.arange(T)[:, None], top_idx].set(top_vals)
        scores = jax.nn.sigmoid(scores.astype(jnp.float32)).astype(logits.dtype)
        xr = x[None, :, :] * scores.T[:, :, None]
        gate_up = jnp.einsum('eth,ehf->etf', xr, gate_up_proj)
        gate, up = jnp.split(gate_up, 2, axis=-1)
        routed = jnp.einsum('etf,efh->eth', up * jax.nn.silu(gate), down_proj)
        routed_sum = routed.sum(axis=0)
        shared = jax.nn.silu(x @ shared_gate_w) * (x @ shared_up_w) @ shared_down_w
        return (shared + routed_sum).reshape(orig_shape)
    x = L0_attn_x
    xn = _layernorm(x, axis=-1)
    s = _L0_attn_ref(xn, L0_attn_Wq, L0_attn_bq, L0_attn_Wk, L0_attn_bk, L0_attn_Wv, L0_attn_bv)
    g = _silu(_L0_ffn_ref(xn, L0_ffn_router_w, L0_ffn_gate_up_proj, L0_ffn_down_proj, L0_ffn_shared_gate_w, L0_ffn_shared_up_w, L0_ffn_shared_down_w))
    x = x + s * g
    return x

_drawn_inputs = setup_inputs


def setup_inputs(seed=0):
    import zlib

    import numpy as np

    out = dict(_drawn_inputs(seed))
    spreads = {'L0_attn_bq': (0.0, 0.8), 'L0_attn_bk': (0.0, 0.8), 'L0_attn_bv': (0.0, 0.8)}
    factors = {'L0_attn_Wq': 8.0,
     'L0_attn_Wk': 8.0,
     'L0_attn_Wv': 8.0,
     'L0_ffn_router_w': 8.0,
     'L0_ffn_gate_up_proj': 8.0,
     'L0_ffn_down_proj': 8.0,
     'L0_ffn_shared_gate_w': 4.722,
     'L0_ffn_shared_up_w': 4.683,
     'L0_ffn_shared_down_w': 4.657}
    for name, (base, spread) in spreads.items():
        noise = np.random.default_rng([zlib.crc32(name.encode()), seed]).standard_normal(out[name].shape)
        drawn = base * np.exp(spread * noise) if base else spread * noise
        out[name] = jnp.asarray(drawn.astype(out[name].dtype))
    for name, factor in factors.items():
        out[name] = (out[name] * factor).astype(out[name].dtype)
    return out
```

```python
from contextlib import ExitStack

import concourse.bass as bass
from concourse import mybir

F32, F32R, I32 = mybir.dt.float32, mybir.dt.float32r, mybir.dt.int32
ACT = mybir.ActivationFunctionType
ALU = mybir.AluOpType
AX = mybir.AxisListType

P = 128
B, N, D, H = 16, 256, 256, 16
DH = D // H
T = B * N
TT = T // P
KD = D // P
E, F = 8, 512
KF = F // P
SLOTS = TT + E - 1
UH = 8
UNITS = B * H // UH
UW = UH * N
RING = 4
EPS = 1e-5
SPLIT_ROWS = 3 * DH
MROW = 64
PAIRS = B // 2
ZT = 4
SBUF_END = 229344


def wait(eng, sem, value):
    if not isinstance(value, int) or value > 0:
        eng.wait_ge(sem, value)


def build(nc, x, wq, wk, wv, bq, bk, bv, rw, wgu, wdn, wsg, wsu, wsd, out):
    ctx = ExitStack()
    with ctx:
        at = [16512]

        def sb(name, shape, dt=F32):
            n = 4
            for k in shape[1:]:
                n *= k
            t = nc.alloc_sbuf_tensor_at(name, shape, dt, offset=at[0])
            at[0] += (n + 31) // 32 * 32
            assert at[0] <= SBUF_END, (name, at[0])
            return t

        def sem(name):
            return ctx.enter_context(nc.semaphore(name))

        xn_d = nc.dram_tensor("xn_d", [T, D], F32, kind="Internal").ap()
        xs_d = nc.dram_tensor("xs_d", [SLOTS * P, D], F32, kind="Internal").ap()
        ys_d = nc.dram_tensor("ys_d", [SLOTS * P, D], F32, kind="Internal").ap()
        s_d = nc.dram_tensor("s_d", [T, D], F32, kind="Internal").ap()
        qk_d = nc.dram_tensor("qk_d", [UNITS, 2, 2, P, N], F32, kind="Internal").ap()

        ident = sb("ident", [P, P])
        score = sb("score", [P, TT])
        dest = sb("dest", [P, TT], I32)
        eid = sb("eid", [1, SLOTS + 1], I32)
        late_at = at[0]
        late = sb("late", [P, 3 * 1024])
        SG = late[:, 0:KD * 2 * F].rearrange("p (k f) -> p k f", k=KD)
        SD = late[:, KD * 2 * F:].rearrange("p (k f) -> p k f", k=KF)
        PT = late[:, 0:2048].rearrange("p (k c) -> p k c", k=2)
        xst = late[:, 2048:3072].rearrange("p (s j c) -> p s j c", s=2, j=2)
        wg_at = at[0]
        WG = sb("WG", [P, E, KD, 2 * F])
        WD = sb("WD", [P, E, KF, D])
        stage_at = at[0]

        at[0] = wg_at
        x_all = sb("x_all", [P, TT, D])
        xnr = sb("xnr", [P, 4, D])
        xT0 = sb("xT0", [P, 4, KD, P])
        zero = sb("zero", [P, D])
        stats = sb("stats", [P, TT, 6])
        mv = sb("mv", [P, TT, 2])
        mean = sb("mean", [P, TT])
        var = sb("var", [P, TT])
        root = sb("root", [P, TT])
        rstd = sb("rstd", [P, TT])
        tmp = sb("tmp", [P, TT])
        lg = sb("lg", [P, TT, E])
        oh = sb("oh", [P, TT, E])
        em8 = sb("em8", [P, TT, E])
        cand = sb("cand", [P, TT, E])
        incl = sb("incl", [P, TT, E])
        em8i = sb("em8i", [P, TT, E], I32)
        steps_i = sb("steps_i", [P, E, TT], I32)
        steps = sb("steps", [P, E, TT])
        slot_i = sb("slot_i", [P, SLOTS + 1, E], I32)
        slot_f = sb("slot_f", [P, SLOTS + 1, E])
        before = sb("before", [P, P])
        ones = sb("ones", [P, P])
        nt = sb("nt", [P, E])
        tend = sb("tend", [P, E])
        base = sb("base", [P, E])
        destf = sb("destf", [P, TT])
        eidf = sb("eidf", [P, SLOTS + 1])
        assert at[0] <= stage_at

        at[0] = stage_at
        QP = [sb(f"QP{w}", [P, UW], F32R) for w in range(RING)]
        KP = [sb(f"KP{w}", [P, UW], F32R) for w in range(RING)]
        stag = sb("stag", [P, 2, 2, N], F32R)
        xa = sb("xa", [P, 2, 2, D])
        xT = sb("xT", [P, 2, KD, N])
        V = sb("V", [P, 2, 2, H, 2 * DH])
        WQKV = sb("WQKV", [P, 3, KD, D])
        RW = sb("RW", [P, KD, E])
        bqk = sb("bqk", [P, 2, 2])
        bvb = sb("bvb", [P, D])
        OTs = sb("OTs", [P, 2, N])
        rden = sb("rden", [P, 16])
        sst = sb("sst", [P, 2, D])
        xr = sb("xr", [P, 2, D])
        idx2 = sb("idx2", [P, 2], I32)
        mx = sb("mx", [P, 2, UH, 2])
        mm = sb("mm", [16, 2, P], F32R)

        at[0] = stage_at
        xin = sb("xin", [P, 2, D])
        xTf = sb("xTf", [P, 2, KD, P])
        sgb = sb("sgb", [P, 2, F])
        hb = sb("hb", [P, 2, F])
        hTs = sb("hTs", [P, 2, KF, P])
        yb = sb("yb", [P, 2, D])
        rb = sb("rb", [P, 2, D])
        sl = sb("sl", [P, 2, D])
        xl = sb("xl", [P, 2, D])
        gz = sb("gz", [P, 2, D])
        o1 = sb("o1", [P, 2, D])
        ob = sb("ob", [P, 2, D])
        idx3 = sb("idx3", [P, 2], I32)

        ps = ctx.enter_context(nc.psum_tensor("ps", [P, 8, 512], F32))
        SA = [ps[:, 2 * a:2 * a + 2, :].rearrange("p b (h k) -> p (b h) k", k=N) for a in range(2)]
        ST, PV, MISC = 4, 6, 7

        x_in = [sem(f"x_in{c}") for c in range(4)]
        const_in = sem("const_in")
        zero_set, zero_out = sem("zero_set"), sem("zero_out")
        pool_const, link, var_done, root_done = sem("pool_const"), sem("link"), sem("var_done"), sem("root_done")
        xn_ready, xn_out = sem("xn_ready"), sem("xn_out")
        tr_ready, tr_copied, lg_ready = sem("tr_ready"), sem("tr_copied"), sem("lg_ready")
        oh_ready, rank_ready, neg_max, exp_max, routed = (sem("oh_ready"), sem("rank_ready"), sem("neg_max"),
                                                          sem("exp_max"), sem("routed"))
        pads_set = sem("pads_set")
        xst_in, xa_in = [sem(f"xst_in{p}") for p in range(2)], [sem(f"xa_in{p}") for p in range(2)]
        xt_ready, xt_copied = sem("xt_ready"), sem("xt_copied")
        qk_ready, qk_hi, qk_lo = sem("qk_ready"), sem("qk_hi"), sem("qk_lo")
        qk_out = [sem(f"qk_out{w}") for w in range(RING)]
        packed = [sem(f"packed{w}") for w in range(RING)]
        v_ready, v_copied = sem("v_ready"), sem("v_copied")
        s_ready, s_reduced = sem("s_ready"), sem("s_reduced")
        mt_ready, m_hi, m_lo = sem("mt_ready"), sem("m_hi"), sem("m_lo")
        m_in = [sem(f"m_in{w}") for w in range(RING)]
        st_ready, exp_done, pv_done, o_copied = sem("st_ready"), sem("exp_done"), sem("pv_done"), sem("o_copied")
        ot_ready, inv_done, normed, s_added, s_out = (sem("ot_ready"), sem("inv_done"), sem("normed"), sem("s_added"),
                                                      sem("s_out"))
        xr_ready, scattered = sem("xr_ready"), [sem(f"scattered{j}") for j in range(2)]
        wg_in, sh_in = sem("wg_in"), sem("sh_in")
        xin_in = [sem(f"xin_in{p}") for p in range(2)]
        xf_ready, xf_copied = sem("xf_ready"), sem("xf_copied")
        gate_ready, up_ready, silu_done, h_done = sem("gate_ready"), sem("up_ready"), sem("silu_done"), sem("h_done")
        ht_ready, ht_copied, y_ready, y_copied = sem("ht_ready"), sem("ht_copied"), sem("y_ready"), sem("y_copied")
        y_out = [sem(f"y_out{p}") for p in range(2)]
        idx_set = sem("idx_set")
        batches_sent, tiles_fetched = sem("batches_sent"), sem("tiles_fetched")
        r_in, fin_in = [sem(f"r_in{p}") for p in range(2)], [sem(f"fin_in{p}") for p in range(2)]
        z_silu, gated, o_done = sem("z_silu"), sem("gated"), sem("o_done")
        o_out = [sem(f"o_out{p}") for p in range(2)]

        block = ctx.enter_context(nc.Block())

        def tiles4(eng, body):
            body(0)
            with eng.Fori(1, TT // 4) as i:
                body(i)

        def pairs(eng, body):
            body(0)
            with eng.Fori(1, PAIRS - 1) as i:
                body(i)
            body(PAIRS - 1)

        def count(i, w, per=1, extra=0):
            return i * (RING * per) + (w * per + extra)

        def exists(i, w, ahead):
            return not isinstance(i, int) or RING * i + w + ahead < UNITS

        def slot_use(i, w):
            return w % RING, i + (w // RING + 1)

        FIRST_SHARED, TURNS = SLOTS, SLOTS + TT

        def turns(body):
            def flat(q, kind, last, nxt):
                body(q // 2, q % 2, kind, last, nxt)
            R, S = "routed", "shared"
            flat(0, R, None, R)
            flat(1, R, R, R)
            flat(2, R, R, R)
            with body.engine.Fori(1, (SLOTS - 2) // 2) as i:
                body(i, 1, R, R, R)
                body(i + 1, 0, R, R, R)
            for q in range(3 + 2 * ((SLOTS - 2) // 2 - 1), SLOTS - 1):
                flat(q, R, R, R)
            flat(SLOTS - 1, R, R, S)
            flat(SLOTS, S, R, S)
            flat(SLOTS + 1, S, S, S)
            flat(SLOTS + 2, S, S, S)
            h0 = (SLOTS + 3) // 2
            with body.engine.Fori(h0, h0 + (TT - 4) // 2) as i:
                body(i, 0, S, S, S)
                body(i, 1, S, S, S)
            flat(TURNS - 1, S, S, None)
            flat(TURNS, None, S, None)

        def q_of(h, p):
            return h * 2 + p

        def before_turn(h, p):
            return (h, 0) if p else (h - 1, 1)

        def shared_use(h, p):
            return h - ((SLOTS + 1 - p) // 2 - 1)

        @block.sync
        def _(sp):
            xv = x.rearrange("(t p) c -> p t c", p=P)
            for c in range(4):
                sp.dma_start(x_all[:, 8 * c:8 * c + 8, :], xv[:, 8 * c:8 * c + 8, :]).then_inc(x_in[c], 16)
            for a, w in enumerate((wq, wk, wv)):
                sp.dma_start(WQKV[:, a, :, :], w.rearrange("(k p) c -> p k c", p=P)).then_inc(const_in, 16)
            sp.dma_start(RW[:, :, :], rw.rearrange("(k p) e -> p k e", p=P)).then_inc(const_in, 16)
            for a, w in enumerate((bq, bk)):
                sp.dma_start(bqk[:, a, :], w).then_inc(const_in, 16)
            sp.dma_start(bvb[:, :], bv.broadcast_to([P, D])).then_inc(const_in, 16)
            sp.wait_ge(zero_set, 1)
            for s in range(SLOTS):
                sp.dma_start(xs_d[s * P:(s + 1) * P, :], zero[:, :]).then_inc(zero_out, 16)

            def store_xn(i):
                sp.wait_ge(xn_ready, i * 4 + 4)
                sp.dma_start(xn_d[bass.ds(i * (4 * P), 4 * P), :].rearrange("(t p) c -> p t c", p=P),
                             xnr[:, :, :]).then_inc(xn_out, 16)
            tiles4(sp, store_xn)
            sp.wait_ge(xn_out, 16 * (TT // 4))

            def rows(b, parity, dst, done):
                sp.dma_start(dst[:, parity, :, :], xn_d[bass.ds(b * N, N), :].rearrange("(j p) c -> p j c", p=P))\
                  .then_inc(done[parity], 16)

            def store_qk(i, w):
                s, _ = slot_use(i, w)
                sp.wait_ge(qk_hi, count(i, w, 1, 1))
                sp.wait_ge(qk_lo, count(i, w, 1, 1))
                sp.dma_start(qk_d[bass.ds(count(i, w), 1), :, :, :, :].rearrange("u a l p t -> p (u a l) t"),
                             stag[:, :, :, :].rearrange("p a l t -> p (a l) t").bitcast(F32)).then_inc(qk_out[s], 16)

            def pack(i, w):
                s, use = slot_use(i, w)
                u, stored, used = count(i, w), use * 16, count(i, w, 4, -4 * (RING - 1))
                if not isinstance(i, int):
                    used, stored = sp.to_reg(used), sp.to_reg(stored)
                wait(sp, pv_done, used)
                sp.wait_ge(qk_out[s], stored)

                def part(a, l0, l1):
                    return qk_d[bass.ds(u, 1), a, l0:l1, :, :].rearrange("u l (d h) t -> (u l d) (h t)", h=UH)
                sp.dma_start(QP[s][0:2 * DH, :].bitcast(F32), part(0, 0, 2)).then_inc(packed[s], 16)
                sp.dma_start(QP[s][2 * DH:3 * DH, :].bitcast(F32), part(0, 0, 1)).then_inc(packed[s], 16)
                sp.dma_start(KP[s][0:DH, :].bitcast(F32), part(1, 0, 1)).then_inc(packed[s], 16)
                sp.dma_start(KP[s][DH:3 * DH, :].bitcast(F32), part(1, 0, 2)).then_inc(packed[s], 16)

            def max_rows(i, w):
                s, _ = slot_use(i, w)
                sp.wait_ge(m_hi, count(i, w, 1, 1))
                sp.wait_ge(m_lo, count(i, w, 1, 1))
                for l in range(2):
                    sp.dma_start(QP[s][MROW + l:MROW + l + 1, :].bitcast(F32).rearrange("o (r q) -> o r q", q=P),
                                 mm[:, l, :].bitcast(F32)).then_inc(m_in[s], 16)

            for b in range(2):
                rows(b, b, xst, xst_in)
            rows(0, 0, xa, xa_in)
            sp.wait_ge(pads_set, 2 * RING)
            for w in range(RING):
                store_qk(0, w)
                if w < 3:
                    pack(0, w)
            max_rows(0, 0)

            def step(i, w):
                m, b = w % 2, i * 2 + w // 2
                if m == 0 and exists(i, w, 4):
                    sp.wait_ge(xt_ready, b + 1)
                    rows(b + 2, w // 2, xst, xst_in)
                if exists(i, w, 3):
                    pack(i, w + 3)
                if exists(i, w, 1):
                    max_rows(i, w + 1)
                if m == 0:
                    wait(sp, s_added, count(i, w, 1, 0))
                    if not (isinstance(i, int) and RING * i + w == 0):
                        store_s(b - 1)
                    if exists(i, w, 2):
                        rows(b + 1, (w // 2 + 1) % 2, xa, xa_in)
                if exists(i, w, 4):
                    store_qk(i, w + 4)

            def store_s(b):
                sp.dma_start(s_d[bass.ds(b * N, N), :].rearrange("(j p) c -> p j c", p=P), sst[:, :, :])\
                  .then_inc(s_out, 16)

            def body(i):
                for w in range(RING):
                    step(i, w)
            pairs(sp, body)
            sp.wait_ge(s_added, UNITS)
            store_s(B - 1)
            sp.wait_ge(pv_done, 4 * UNITS)
            for h, w in enumerate((wsg, wsu)):
                sp.dma_start(SG[:, :, h * F:(h + 1) * F], w.rearrange("(k p) f -> p k f", p=P)).then_inc(sh_in, 16)
            sp.dma_start(SD[:, :, :], wsd.rearrange("(k p) c -> p k c", p=P)).then_inc(sh_in, 16)
            for j in range(2):
                sp.wait_ge(scattered[j], 16 * B)
            sp.wait_ge(s_out, 16 * B)

            def load_in(h, p, kind):
                row = q_of(h, p) * P if kind == "routed" else q_of(h, p) * P - FIRST_SHARED * P
                src = xs_d if kind == "routed" else xn_d
                sp.dma_start(xin[:, p, :], src[bass.ds(row, P), :]).then_inc(xin_in[p], 16)

            load_in(0, 0, "routed")

            def turn(h, p, kind, last, nxt):
                q, (h1, p1) = q_of(h, p), before_turn(h, p)
                if nxt:
                    wait(sp, xf_ready, q)
                    load_in(*((h, 1) if p == 0 else (h + 1, 0)), nxt)
                if kind == "shared":
                    row = q * P - FIRST_SHARED * P
                    wait(sp, o_done, q - (FIRST_SHARED + 1))
                    sp.dma_start(sl[:, p, :], s_d[bass.ds(row, P), :]).then_inc(fin_in[p], 16)
                    sp.dma_start(xl[:, p, :], x[bass.ds(row, P), :]).then_inc(fin_in[p], 16)
                if last == "routed":
                    sp.wait_ge(y_copied, q)
                    sp.dma_start(ys_d[bass.ds(q * P - P, P), :], yb[:, p1, :]).then_inc(y_out[p1], 16)
                if last == "shared":
                    sp.wait_ge(o_done, q - FIRST_SHARED)
                    sp.dma_start(out[bass.ds(q * P - (1 + FIRST_SHARED) * P, P), :], ob[:, p1, :])\
                      .then_inc(o_out[p1], 16)
            turn.engine = sp
            turns(turn)
            for p in range(2):
                sp.wait_ge(o_out[p], 16 * TT // 2)

        @block.gpsimd
        def _(pool):
            g = nc.gpsimd
            g.memset(zero[:, :], 0.0).then_inc(zero_set, 1)
            g.memset(ident[:, :], 0.0).then_inc(pool_const, 1)
            g.memset(before[:, :], 1.0).then_inc(pool_const, 1)
            g.memset(ones[:, :], 1.0).then_inc(pool_const, 1)
            g.iota(em8i[:, :, :], pattern=[[0, TT], [1, E]], base=-E, channel_multiplier=0).then_inc(pool_const, 1)
            g.iota(steps_i[:, :, :], pattern=[[0, E], [P, TT]], base=0, channel_multiplier=0).then_inc(pool_const, 1)
            g.iota(slot_i[:, :, :], pattern=[[1, SLOTS + 1], [0, E]], base=0, channel_multiplier=0)\
             .then_inc(pool_const, 1)
            pool.wait_ge(pool_const, 6)
            g.affine_select(out=ident[:, :], in_=ident[:, :], compare_op=ALU.not_equal, fill=1.0, base=0,
                            pattern=[[-1, P]], channel_multiplier=1).then_inc(pool_const, 1)
            g.affine_select(out=before[:, :], in_=before[:, :], compare_op=ALU.is_gt, fill=0.0, base=0,
                            pattern=[[1, P]], channel_multiplier=-1).then_inc(pool_const, 1)
            g.memset(V[:, :, :, :, DH:].rearrange("p a b h c -> p (a b h) c"), 0.0)
            for w in range(RING):
                g.memset(QP[w][:, :].bitcast(F32), 0.0).then_inc(pads_set, 1)
                g.memset(KP[w][:, :].bitcast(F32), 0.0).then_inc(pads_set, 1)
            pool.wait_ge(pads_set, 2 * RING)
            g.memset(V[:, :, :, :, DH:DH + 1].rearrange("p a b h c -> p (a b h) c"), 1.0).then_inc(pads_set, 1)
            pool.wait_ge(pads_set, 2 * RING + 1)
            for w in range(RING):
                g.memset(KP[w][MROW:MROW + 2, :].bitcast(F32), 1.0).then_inc(pads_set, 1)
            pool.wait_ge(pads_set, 3 * RING + 1)

            pool.wait_ge(routed, 1)
            pool.wait_ge(xn_out, 16 * (TT // 4))
            pool.wait_ge(zero_out, 16 * SLOTS)
            for e in range(E):
                pool.dma_start(WG[:, e, :, :], wgu[e].rearrange("(k p) f -> p k f", p=P)).then_inc(wg_in, 16)
                pool.dma_start(WD[:, e, :, :], wdn[e].rearrange("(k p) c -> p k c", p=P)).then_inc(wg_in, 16)

            def scatter(i, w):
                b, par = i * 2 + w // 2, (w // 2) % 2
                pool.wait_ge(xa_in[par], i * 16 + 16)
                for j in range(2):
                    wait(pool, scattered[j], b * 16)
                    g.tensor_copy(idx2[:, j:j + 1], dest[:, bass.ds(b * 2 + j, 1)]).then_inc(xr_ready, 1)
                    g.tensor_tensor(xr[:, j, :], xa[:, par, j, :],
                                    score[:, bass.ds(b * 2 + j, 1)].to_broadcast([P, D]), ALU.mult).then_inc(xr_ready, 1)
                pool.wait_ge(xr_ready, b * 4 + 4)
                pool.sem_inc(batches_sent, 1)
                for j in range(2):
                    g.indirect_dma_start(out=xs_d, out_offset=bass.IndirectOffsetOnAxis(ap=idx2[:, j:j + 1], axis=0),
                                         in_=xr[:, j, :], in_offset=None).then_inc(scattered[j], 16)

            def add_xn(i, w):
                m, par = w % 2, (w // 2) % 2
                pool.wait_ge(normed, count(i, w, 1, 1))
                cols = slice(P * m, P * m + P)
                g.tensor_tensor(sst[:, :, cols], sst[:, :, cols], xa[:, par, :, cols], ALU.add).then_inc(s_added, 1)

            def body(i):
                for w in range(RING):
                    if w % 2 == 0:
                        scatter(i, w)
                    if not (isinstance(i, int) and i == 0 and w == 0):
                        add_xn(i, w - 1)
            pairs(pool, body)
            add_xn(PAIRS, -1)

            def turn(h, p, kind, last, nxt):
                q, (h1, p1) = q_of(h, p), before_turn(h, p)
                if kind == "shared":
                    if isinstance(q, int) and q == FIRST_SHARED:
                        for k in range(2):
                            pool.wait_ge(y_out[k], 16 * ((SLOTS + 1 - k) // 2))
                    pool.wait_ge(y_copied, q - 1)
                    g.tensor_copy(idx3[:, p:p + 1], dest[:, bass.ds(q - FIRST_SHARED, 1)]).then_inc(idx_set, 1)
                    pool.wait_ge(idx_set, q - (FIRST_SHARED - 1))
                    pool.sem_inc(tiles_fetched, 1)
                    g.indirect_dma_start(out=rb[:, p, :], out_offset=None, in_=ys_d,
                                         in_offset=bass.IndirectOffsetOnAxis(ap=idx3[:, p:p + 1], axis=0))\
                     .then_inc(r_in[p], 16)
                if last == "shared":
                    use = shared_use(h1, p1)
                    pool.wait_ge(z_silu, q - FIRST_SHARED)
                    pool.wait_ge(fin_in[p1], use * 32)
                    g.tensor_tensor(o1[:, p1, :], gz[:, p1, :], sl[:, p1, :], ALU.mult).then_inc(gated, 1)
                    pool.wait_ge(gated, q - FIRST_SHARED)
                    wait(pool, o_out[p1], use * 16 - 16)
                    g.tensor_tensor(ob[:, p1, :], o1[:, p1, :], xl[:, p1, :], ALU.add).then_inc(o_done, 1)
            turn.engine = pool
            turns(turn)

        @block.scalar
        def _(act):
            a_ = nc.scalar
            act.wait_ge(var_done, 1)
            a_.activation(root[:, :], var[:, :], ACT.Sqrt).then_inc(root_done, 1)

            def copy_t(i):
                for j in range(4):
                    act.wait_ge(tr_ready, i * 4 + j + 1)
                    wait(act, lg_ready, i * 4 + j - 3)
                    a_.activation(xT0[:, j, :, :].rearrange("p k c -> p (k c)"), ps[:, j, 0:N], ACT.Copy)\
                      .then_inc(tr_copied, 1)
            tiles4(act, copy_t)
            act.wait_ge(neg_max, 1)
            a_.activation(score[:, :], tmp[:, :], ACT.Exp, scale=-1.0).then_inc(exp_max, 1)

            def xt_copy(b, par):
                act.wait_ge(xt_ready, b + 1)
                a_.activation(xT[:, par, :, :].rearrange("p k c -> p (k c)"), ps[:, MISC, :], ACT.Copy)\
                  .then_inc(xt_copied, 1)

            def hi_parts(i, w):
                act.wait_ge(qk_ready, count(i, w, 1, 1))
                if not (isinstance(i, int) and RING * i + w == 0):
                    s, use = slot_use(i, w - 1) if w % RING else (RING - 1, i + w // RING)
                    act.wait_ge(qk_out[s], use * 16)
                for a in range(2):
                    ins = a_.activation(stag[:, a, 0, :], ps[:, MISC, a * N:(a + 1) * N], ACT.Identity,
                                        bias=bqk[:, a, w % 2:w % 2 + 1])
                ins.then_inc(qk_hi, 1)

            def max_hi(i, w):
                act.wait_ge(mt_ready, count(i, w, 1, 1))
                if not (isinstance(i, int) and RING * i + w == 0):
                    s, use = slot_use(i, w - 1) if w % RING else (RING - 1, i + w // RING)
                    act.wait_ge(m_in[s], use * 32)
                a_.mul(mm[:, 0, :], ps[0:16, MISC, 0:P], -1.0).then_inc(m_hi, 1)

            act.wait_ge(const_in, 16 * 7)
            xt_copy(0, 0)
            hi_parts(0, 0)
            hi_parts(0, 1)
            xt_copy(1, 1)
            hi_parts(0, 2)
            hi_parts(0, 3)
            max_hi(0, 0)

            def exps(i, w, c):
                gr, kt, hp = c // 4, c // 2 % 2, c % 2
                act.wait_ge(st_ready, count(i, w, 8, c + 1))
                if hp == 0:
                    wait(act, pv_done, count(i, w, 4, 2 * gr + kt - 1))
                a_.activation(PT[:, kt, hp * 512:hp * 512 + 512], ps[:, ST + c % 2, :], ACT.Exp,
                              scale=DH ** -0.5).then_inc(exp_done, 1)

            def o_copy(i, w, gr):
                act.wait_ge(pv_done, count(i, w, 4, 2 * gr + 2))
                wait(act, ot_ready, count(i, w, 1, 0))
                a_.activation(OTs[:, gr, :], ps[:, PV, 0:N], ACT.Copy).then_inc(o_copied, 1)

            def step(i, w):
                for c in range(4):
                    exps(i, w, c)
                if exists(i, w, 1):
                    max_hi(i, w + 1)
                exps(i, w, 4)
                exps(i, w, 5)
                o_copy(i, w, 0)
                if w % 2 == 0 and exists(i, w, 4):
                    xt_copy(i * 2 + (w // 2 + 2), w // 2)
                exps(i, w, 6)
                exps(i, w, 7)
                if exists(i, w, 4):
                    hi_parts(i, w + 4)
                o_copy(i, w, 1)

            def body(i):
                for w in range(RING):
                    step(i, w)
            pairs(act, body)

            def xf_copy(h, p):
                q = q_of(h, p)
                act.wait_ge(xf_ready, q + 1)
                wait(act, up_ready, q - 1)
                a_.activation(xTf[:, p, :, :].rearrange("p k c -> p (k c)"), ps[:, 5, 0:D], ACT.Copy)\
                  .then_inc(xf_copied, 1)
            xf_copy(0, 0)

            def turn(h, p, kind, last, nxt):
                q, (h1, p1) = q_of(h, p), before_turn(h, p)
                if kind:
                    act.wait_ge(gate_ready, q + 1)
                    wait(act, h_done, q - 1)
                    a_.activation(sgb[:, p, :], ps[:, 2 * p, :], ACT.Silu).then_inc(silu_done, 1)
                if nxt:
                    xf_copy(*((h, 1) if p == 0 else (h + 1, 0)))
                if last == "shared":
                    act.wait_ge(y_copied, q)
                    a_.activation(gz[:, p1, :], yb[:, p1, :], ACT.Silu).then_inc(z_silu, 1)
            turn.engine = act
            turns(turn)

        @block.vector
        def _(dve):
            v = nc.vector
            done = [0]

            def chain(ins):
                done[0] += 1
                ins.then_inc(link, 1)
                dve.wait_ge(link, done[0])

            for c in range(4):
                dve.wait_ge(x_in[c], 16)
                for t in range(8 * c, 8 * c + 8):
                    ins = v.bn_stats(stats[:, t, :], x_all[:, t, :])
            chain(ins)
            for t in range(TT):
                ins = v.bn_aggr(mv[:, t, :], stats[:, t, :])
            chain(ins)
            v.tensor_copy(mean[:, :], mv[:, :, 0])
            v.tensor_scalar(var[:, :], mv[:, :, 1], EPS, None, ALU.add).then_inc(var_done, 1)
            dve.wait_ge(root_done, 1)
            chain(v.reciprocal(rstd[:, :], root[:, :]))
            chain(v.tensor_tensor(tmp[:, :], rstd[:, :], rstd[:, :], ALU.mult))
            chain(v.tensor_tensor(tmp[:, :], tmp[:, :], var[:, :], ALU.mult))
            chain(v.tensor_scalar(tmp[:, :], tmp[:, :], -0.5, 1.5, ALU.mult, ALU.add))
            chain(v.tensor_tensor(rstd[:, :], rstd[:, :], tmp[:, :], ALU.mult))

            def normalise(i):
                for j in range(4):
                    wait(dve, tr_ready, i * 4 + j - 3)
                    if j == 0:
                        wait(dve, xn_out, i * 16)
                    v.tensor_scalar(xnr[:, j, :], x_all[:, bass.ds(i * 4 + j, 1), :], mean[:, bass.ds(i * 4 + j, 1)],
                                    rstd[:, bass.ds(i * 4 + j, 1)], ALU.subtract, ALU.mult).then_inc(xn_ready, 1)
            tiles4(dve, normalise)

            dve.wait_ge(pool_const, 8)
            v.tensor_copy(em8[:, :, :], em8i[:, :, :])
            v.tensor_copy(steps[:, :, :], steps_i[:, :, :])
            v.tensor_copy(slot_f[:, :, :], slot_i[:, :, :])
            dve.wait_ge(lg_ready, TT)
            chain(v.tensor_copy(lg[:, :, :].rearrange("p t e -> p (t e)"), ps[:, MISC, 0:TT * E]))
            chain(v.reduce_max(tmp[:, :], lg[:, :, :], AX.X))
            dve.sem_inc(neg_max, 1)
            chain(v.tensor_tensor(oh[:, :, :], lg[:, :, :], tmp[:, :].rearrange("p (t o) -> p t o", o=1)
                                  .to_broadcast([P, TT, E]), ALU.is_equal))
            chain(v.tensor_tensor(cand[:, :, :], oh[:, :, :], em8[:, :, :], ALU.mult))
            chain(v.tensor_reduce(mean[:, :], cand[:, :, :], AX.X, ALU.min))
            v.tensor_tensor(oh[:, :, :], em8[:, :, :], mean[:, :].rearrange("p (t o) -> p t o", o=1)
                            .to_broadcast([P, TT, E]), ALU.is_equal).then_inc(oh_ready, 1)
            dve.wait_ge(exp_max, 1)
            chain(v.tensor_scalar(score[:, :], score[:, :], 1.0, None, ALU.add))
            chain(v.reciprocal(score[:, :], score[:, :]))
            dve.wait_ge(rank_ready, 1)
            chain(v.tensor_copy(cand[:, :, :].rearrange("p t e -> p (t e)"), ps[:, ST + 1, 0:TT * E]))
            chain(v.memset(lg[:, :, 0], 1.0))
            for e in range(E):
                ins = v.tensor_tensor_scan(incl[:, :, e], lg[:, :, 0], cand[:, :, e], 0.0, ALU.mult, ALU.add)
            chain(ins)
            chain(v.tensor_tensor(steps[:, :, :], incl[:, TT - 1, :].rearrange("p (e o) -> p e o", o=1)
                                  .to_broadcast([P, E, TT]), steps[:, :, :], ALU.is_gt))
            chain(v.reduce_sum(nt[:, :], steps[:, :, :], AX.X))
            chain(v.tensor_tensor_scan(tend[:, :], lg[:, 0:E, 0], nt[:, :], 0.0, ALU.mult, ALU.add))
            chain(v.tensor_tensor(base[:, :], tend[:, :], nt[:, :], ALU.subtract))
            chain(v.tensor_scalar(base[:, :], base[:, :], float(P), None, ALU.mult))
            chain(v.tensor_tensor(incl[:, :, :], incl[:, :, :], cand[:, :, :], ALU.subtract))
            chain(v.tensor_tensor(incl[:, :, :], incl[:, :, :], base[:, :].rearrange("p (o e) -> p o e", o=1)
                                  .to_broadcast([P, TT, E]), ALU.add))
            chain(v.tensor_tensor(incl[:, :, :].rearrange("p t e -> p (t e)"),
                                  incl[:, :, :].rearrange("p t e -> p (t e)"), ps[:, ST, 0:TT * E], ALU.add))
            chain(v.tensor_tensor(incl[:, :, :], incl[:, :, :], oh[:, :, :], ALU.mult))
            chain(v.reduce_sum(destf[:, :], incl[:, :, :], AX.X))
            chain(v.tensor_copy(dest[:, :], destf[:, :]))
            chain(v.tensor_tensor(slot_f[:, :, :], slot_f[:, :, :], tend[:, :].rearrange("p (o e) -> p o e", o=1)
                                  .to_broadcast([P, SLOTS + 1, E]), ALU.is_ge))
            chain(v.reduce_sum(eidf[:, :], slot_f[:, :, :], AX.X))
            chain(v.tensor_scalar(eidf[:, :], eidf[:, :], float(E - 1), None, ALU.min))
            v.tensor_copy(eid[0:1, :], eidf[0:1, :]).then_inc(routed, 1)

            def lo_parts(i, w):
                dve.wait_ge(qk_hi, count(i, w, 1, 1))
                for a in range(2):
                    ins = v.scalar_tensor_tensor(stag[:, a, 1, :], ps[:, MISC, a * N:(a + 1) * N],
                                                 bqk[:, a, w % 2:w % 2 + 1], stag[:, a, 0, :].bitcast(F32),
                                                 ALU.add, ALU.subtract)
                ins.then_inc(qk_lo, 1)

            def v_copy(n_done, par, j):
                dve.wait_ge(v_ready, n_done)
                v.tensor_tensor(V[:, par, j, :, 0:DH], ps[:, MISC, 0:D].rearrange("p (h d) -> p h d", d=DH),
                                bvb[:, :].rearrange("p (h d) -> p h d", d=DH), ALU.add).then_inc(v_copied, 1)

            def reduce_chunk(i, w, a):
                j, gr = a // 2, a % 2
                dve.wait_ge(s_ready, count(i, w, 4, a + 1))
                v.reduce_max(mx[:, w % 2, 4 * gr:4 * gr + 4, j], SA[a % 2], AX.X).then_inc(s_reduced, 1)

            def max_lo(i, w):
                dve.wait_ge(m_hi, count(i, w, 1, 1))
                v.scalar_tensor_tensor(mm[:, 1, :], ps[0:16, MISC, 0:P], -1.0, mm[:, 0, :].bitcast(F32),
                                       ALU.mult, ALU.subtract).then_inc(m_lo, 1)

            def norm(i, w):
                dve.wait_ge(ot_ready, count(i, w, 1, 1))
                o = ps[:, MISC, :].rearrange("p (g j h c) -> p g j h c", g=2, j=2, h=4)
                v.reciprocal(rden[:, :], ps[:, MISC, :].rearrange("p (r c) -> p r c", c=2 * DH)[:, :, DH])\
                 .then_inc(inv_done, 1)
                dve.wait_ge(inv_done, count(i, w, 1, 1))
                if w % 2 == 0:
                    wait(dve, s_out, (i * 2 + w // 2) * 16)
                inv = rden[:, :].rearrange("p (g j h o) -> p g j h o", g=2, j=2, h=4)
                for gr in range(2):
                    col = P * (w % 2) + 4 * DH * gr
                    ins = v.tensor_tensor(sst[:, :, col:col + 4 * DH].rearrange("p j (h d) -> p j h d", d=DH),
                                          o[:, gr, :, :, 0:DH], inv[:, gr, :, :, :].to_broadcast([P, 2, 4, DH]), ALU.mult)
                ins.then_inc(normed, 1)

            lo_parts(0, 0)
            lo_parts(0, 1)
            dve.wait_ge(pads_set, 3 * RING + 1)
            v_copy(1, 0, 0)
            v_copy(2, 0, 1)
            lo_parts(0, 2)
            lo_parts(0, 3)
            for a in range(4):
                reduce_chunk(0, 0, a)
            max_lo(0, 0)
            for a in range(4):
                reduce_chunk(0, 1, a)

            def step(i, w):
                if exists(i, w, 2):
                    reduce_chunk(i, w + 2, 0)
                if not (isinstance(i, int) and RING * i + w == 0):
                    norm(i, w - 1)
                if exists(i, w, 2):
                    reduce_chunk(i, w + 2, 1)
                if exists(i, w, 1):
                    max_lo(i, w + 1)
                if exists(i, w, 2):
                    reduce_chunk(i, w + 2, 2)
                if exists(i, w, 4):
                    lo_parts(i, w + 4)
                if exists(i, w, 2):
                    reduce_chunk(i, w + 2, 3)
                    v_copy(count(i, w, 1, 3), (w // 2 + 1) % 2, w % 2)

            def body(i):
                for w in range(RING):
                    step(i, w)
            pairs(dve, body)
            norm(PAIRS, -1)

            def turn(h, p, kind, last, nxt):
                q, (h1, p1) = q_of(h, p), before_turn(h, p)
                if last:
                    dve.wait_ge(ht_ready, q)
                    wait(dve, y_ready, q - 2)
                    v.tensor_copy(hTs[:, p1, :, :].rearrange("p k c -> p (k c)"), ps[:, 4, :]).then_inc(ht_copied, 1)
                if kind:
                    dve.wait_ge(silu_done, q + 1)
                    dve.wait_ge(up_ready, q + 1)
                    wait(dve, ht_ready, q - 1)
                    v.tensor_tensor(hb[:, p, :], sgb[:, p, :], ps[:, 2 * p + 1, :], ALU.mult).then_inc(h_done, 1)
                if last:
                    dve.wait_ge(y_ready, q)
                    y = ps[:, 6 + p1, 0:D]
                    if last == "routed":
                        wait(dve, y_out[p1], h1 * 16)
                        v.tensor_copy(yb[:, p1, :], y).then_inc(y_copied, 1)
                    else:
                        if isinstance(q, int) and q <= FIRST_SHARED + 2:
                            for k in range(2):
                                dve.wait_ge(y_out[k], 16 * ((SLOTS + 1 - k) // 2))
                        wait(dve, z_silu, q - (FIRST_SHARED + 2))
                        dve.wait_ge(r_in[p1], shared_use(h1, p1) * 16)
                        v.tensor_tensor(yb[:, p1, :], y, rb[:, p1, :], ALU.add).then_inc(y_copied, 1)
            turn.engine = dve
            turns(turn)

        @block.tensor
        def _(pe):
            mmul = nc.tensor.matmul
            pe.wait_ge(pool_const, 8)
            pe.wait_ge(const_in, 16 * 7)

            def transpose(dst, src):
                return nc.tensor.transpose(dst, src, ident[:, :])

            def logits(i):
                def tr(j):
                    pe.wait_ge(xn_ready, i * 4 + j + 1)
                    wait(pe, tr_copied, i * 4 + j - 3)
                    for k in range(KD):
                        ins = transpose(ps[:, j, k * P:(k + 1) * P], xnr[:, j, k * P:(k + 1) * P])
                    ins.then_inc(tr_ready, 1)

                def lo(j):
                    pe.wait_ge(tr_copied, i * 4 + j + 1)
                    for k in range(KD):
                        ins = mmul(ps[:, MISC, bass.ds((i * 4 + j) * E, E)], xT0[:, j, k, :], RW[:, k, :],
                                   start=(k == 0), stop=(k == KD - 1))
                    ins.then_inc(lg_ready, 1)
                tr(0)
                tr(1)
                lo(0)
                tr(2)
                lo(1)
                tr(3)
                lo(2)
                lo(3)
            tiles4(pe, logits)
            pe.wait_ge(oh_ready, 1)
            hot = oh[:, :, :].rearrange("p t e -> p (t e)")
            mmul(ps[:, ST, 0:TT * E], before[:, :], hot, start=True, stop=True)
            mmul(ps[:, ST + 1, 0:TT * E], ones[:, :], hot, start=True, stop=True).then_inc(rank_ready, 1)
            pe.wait_ge(routed, 1)

            def xt(b, par, nth):
                pe.wait_ge(xst_in[par], nth * 16)
                for j in range(2):
                    for k in range(KD):
                        ins = transpose(ps[:, MISC, k * N + j * P:k * N + (j + 1) * P],
                                        xst[:, par, j, k * P:(k + 1) * P])
                ins.then_inc(xt_ready, 1)

            def qk(i, w, par):
                m = w % 2
                for a in range(2):
                    for k in range(KD):
                        ins = mmul(ps[:, MISC, a * N:(a + 1) * N], WQKV[:, a, k, m * P:(m + 1) * P], xT[:, par, k, :],
                                   start=(k == 0), stop=(k == KD - 1))
                ins.then_inc(qk_ready, 1)

            def v_tile(par, j):
                for k in range(KD):
                    ins = mmul(ps[:, MISC, 0:D], xT[:, par, k, j * P:(j + 1) * P], WQKV[:, 2, k, :],
                               start=(k == 0), stop=(k == KD - 1))
                ins.then_inc(v_ready, 1)

            def scores(i, w, a):
                s, use = slot_use(i, w)
                j, gr = a // 2, a % 2
                if a == 0:
                    pe.wait_ge(packed[s], use * 64)
                wait(pe, s_reduced, count(i, w, 4, a - 1))
                for h in range(4):
                    c = (4 * gr + h) * N
                    ins = mmul(SA[a % 2][:, h, :], QP[s][0:SPLIT_ROWS, c + j * P:c + (j + 1) * P],
                               KP[s][0:SPLIT_ROWS, c:c + N], start=True, stop=True)
                ins.then_inc(s_ready, 1)

            def max_t(i, w):
                pe.wait_ge(s_reduced, count(i, w, 4, 4))
                transpose(ps[0:16, MISC, 0:P], mx[:, w % 2, :, :].rearrange("p h j -> p (h j)")).then_inc(mt_ready, 1)

            def scores_t(i, w, c):
                s, use = slot_use(i, w)
                gr, kt, hp = c // 4, c // 2 % 2, c % 2
                if c == 0:
                    pe.wait_ge(m_in[s], use * 32)
                wait(pe, exp_done, count(i, w, 8, c - 1))
                for h in range(2):
                    col = (4 * gr + 2 * hp + h) * N
                    ins = mmul(ps[:, ST + c % 2, h * N:(h + 1) * N], KP[s][:, col + kt * P:col + (kt + 1) * P],
                               QP[s][:, col:col + N], start=True, stop=True)
                ins.then_inc(st_ready, 1)

            def weighted(i, w, gr, kt):
                pe.wait_ge(exp_done, count(i, w, 8, 4 * gr + 2 * kt + 2))
                if kt == 0:
                    wait(pe, o_copied, count(i, w, 2, gr))
                for h in range(4):
                    head = UH * (w % 2) + 4 * gr + h
                    ins = mmul(ps[32 * h:32 * h + 32, PV, 0:N], V[:, (w // 2) % 2, kt, head, :],
                               PT[:, kt, h * N:(h + 1) * N], start=(kt == 0), stop=(kt == 1),
                               tile_position=(0, 32 * h))
                ins.then_inc(pv_done, 1)

            def out_t(i, w):
                pe.wait_ge(o_copied, count(i, w, 2, 2))
                for gr in range(2):
                    for j in range(2):
                        c = (2 * gr + j) * P
                        ins = transpose(ps[:, MISC, c:c + P], OTs[:, gr, j * P:(j + 1) * P])
                ins.then_inc(ot_ready, 1)

            xt(0, 0, 1)
            pe.wait_ge(xt_copied, 1)
            qk(0, 0, 0)
            pe.wait_ge(qk_lo, 1)
            qk(0, 1, 0)
            pe.wait_ge(qk_lo, 2)
            v_tile(0, 0)
            pe.wait_ge(v_copied, 1)
            v_tile(0, 1)
            pe.wait_ge(v_copied, 2)
            xt(1, 1, 1)
            pe.wait_ge(xt_copied, 2)
            qk(0, 2, 1)
            pe.wait_ge(qk_lo, 3)
            qk(0, 3, 1)
            for a in range(4):
                scores(0, 0, a)
            pe.wait_ge(qk_lo, 4)
            max_t(0, 0)
            for a in range(4):
                scores(0, 1, a)

            def step(i, w):
                m, par = w % 2, w // 2
                first = isinstance(i, int) and RING * i + w == 0
                ahead = exists(i, w, 2)
                if ahead:
                    scores(i, w + 2, 0)
                scores_t(i, w, 0)
                scores_t(i, w, 1)
                if not first:
                    if exists(i, w, 1):
                        pe.wait_ge(v_copied, count(i, w, 1, 2))
                    else:
                        pe.wait_ge(m_lo, count(i, w, 1, 1))
                    out_t(i, w - 1)
                scores_t(i, w, 2)
                scores_t(i, w, 3)
                if ahead:
                    scores(i, w + 2, 1)
                weighted(i, w, 0, 0)
                if exists(i, w, 1):
                    if first:
                        pe.wait_ge(m_lo, 1)
                    else:
                        pe.wait_ge(normed, count(i, w, 1, 0))
                    max_t(i, w + 1)
                scores_t(i, w, 4)
                scores_t(i, w, 5)
                weighted(i, w, 0, 1)
                if ahead:
                    scores(i, w + 2, 2)
                if exists(i, w, 1):
                    pe.wait_ge(m_lo, count(i, w, 1, 2))
                if m == 0 and exists(i, w, 4):
                    xt(None, par, i + 2)
                scores_t(i, w, 6)
                scores_t(i, w, 7)
                weighted(i, w, 1, 0)
                if exists(i, w, 4):
                    if m == 0:
                        pe.wait_ge(xt_copied, i * 2 + (par + 3))
                    qk(i, w + 4, par)
                if ahead:
                    scores(i, w + 2, 3)
                    if exists(i, w, 4):
                        pe.wait_ge(qk_lo, count(i, w, 1, 5))
                    v_tile(1 - par, m)
                weighted(i, w, 1, 1)

            def body(i):
                for w in range(RING):
                    step(i, w)
            pairs(pe, body)
            pe.wait_ge(normed, UNITS - 1)
            out_t(PAIRS, -1)

            def xf(h, p):
                q = q_of(h, p)
                pe.wait_ge(xin_in[p], h * 16 + 16)
                wait(pe, xf_copied, q)
                for k in range(KD):
                    ins = transpose(ps[:, 5, k * P:(k + 1) * P], xin[:, p, k * P:(k + 1) * P])
                ins.then_inc(xf_ready, 1)

            pe.wait_ge(exp_done, 8 * UNITS)
            xf(0, 0)
            pe.wait_ge(wg_in, 2 * 16 * E)
            pe.wait_ge(s_reduced, 4 * UNITS)
            pe.wait_ge(normed, UNITS)

            def turn(h, p, kind, last, nxt):
                q, (h1, p1) = q_of(h, p), before_turn(h, p)

                def gate_up(half, done):
                    for k in range(KD):
                        ws = SG[:, k, half * F:(half + 1) * F] if kind == "shared" else \
                            WG[:, bass.ds(e_now, 1), k, half * F:(half + 1) * F]
                        ins = mmul(ps[:, 2 * p + half, :], xTf[:, p, k, :], ws, start=(k == 0), stop=(k == KD - 1))
                    ins.then_inc(done, 1)
                if kind == "shared" and isinstance(q, int) and q == FIRST_SHARED:
                    pe.wait_ge(sh_in, 3 * 16)
                if kind:
                    if kind == "routed":
                        e_now = pe.value_load(eid[0:1, bass.ds(q, 1)], min_val=0, max_val=E - 1)
                    pe.wait_ge(xf_copied, q + 1)
                    wait(pe, silu_done, q - 1)
                    gate_up(0, gate_ready)
                if last:
                    pe.wait_ge(h_done, q)
                    wait(pe, ht_copied, q - 1)
                    for k in range(KF):
                        ins = transpose(ps[:, 4, k * P:(k + 1) * P], hb[:, p1, k * P:(k + 1) * P])
                    ins.then_inc(ht_ready, 1)
                if kind:
                    wait(pe, h_done, q - 1)
                    gate_up(1, up_ready)
                if nxt:
                    xf(*((h, 1) if p == 0 else (h + 1, 0)))
                if last:
                    if last == "routed":
                        e_last = pe.value_load(eid[0:1, bass.ds(q - 1, 1)], min_val=0, max_val=E - 1)
                    pe.wait_ge(ht_copied, q)
                    wait(pe, y_copied, q - 2)
                    for k in range(KF):
                        ws = SD[:, k, :] if last == "shared" else WD[:, bass.ds(e_last, 1), k, :]
                        ins = mmul(ps[:, 6 + p1, 0:D], hTs[:, p1, k, :], ws, start=(k == 0), stop=(k == KF - 1))
                    ins.then_inc(y_ready, 1)
            turn.engine = pe
            turns(turn)


def kernel(**inputs):
    import numpy as np
    import concourse.bacc as bacc
    from concourse.bass_utils import run_bass_kernel_spmd

    a = {k[3:]: np.asarray(v) for k, v in inputs.items()}

    def by_dim(w):
        return np.ascontiguousarray(w.reshape(w.shape[:-1] + (2, UH, DH)).swapaxes(-1, -2).reshape(w.shape))

    arrays = {
        "x": a["attn_x"].reshape(T, D),
        "wq": by_dim(a["attn_Wq"]), "wk": by_dim(a["attn_Wk"]), "wv": a["attn_Wv"],
        "bq": by_dim(a["attn_bq"]).reshape(2, P).T, "bk": by_dim(a["attn_bk"]).reshape(2, P).T,
        "bv": a["attn_bv"].reshape(1, D), "rw": a["ffn_router_w"].T,
        "wgu": a["ffn_gate_up_proj"], "wdn": a["ffn_down_proj"],
        "wsg": a["ffn_shared_gate_w"], "wsu": a["ffn_shared_up_w"], "wsd": a["ffn_shared_down_w"],
    }
    nc = bacc.Bacc("TRN2", target_bir_lowering=False, num_devices=1)
    maps, args = {}, []
    for name, v in arrays.items():
        v = np.ascontiguousarray(v)
        maps["in_" + name] = v
        args.append(nc.dram_tensor("in_" + name, v.shape, F32, kind="ExternalInput").ap())
    args.append(nc.dram_tensor("out", (T, D), F32, kind="ExternalOutput").ap())
    build(nc, *args)
    r = run_bass_kernel_spmd(nc, [maps], core_ids=[0])
    return r.results[0]["out"].reshape(B, N, D)
```

```python
from contextlib import ExitStack

import concourse.bass as bass
from concourse import mybir

F32, F32R, I32 = mybir.dt.float32, mybir.dt.float32r, mybir.dt.int32
ACT = mybir.ActivationFunctionType
ALU = mybir.AluOpType
AX = mybir.AxisListType

P = 128
B, N, D, H = 16, 256, 256, 16
DH = D // H
T = B * N
TT = T // P
KD = D // P
E, F = 8, 512
KF = F // P
SLOTS = TT + E - 1
UH = 8
UNITS = B * H // UH
UW = UH * N
RING = 4
EPS = 1e-5
SPLIT_ROWS = 3 * DH
MROW = 64
PAIRS = B // 2
ZT = 3
AHEAD = 5
GT = 8
SBUF_END = 229344


def wait(eng, sem, value):
    if not isinstance(value, int) or value > 0:
        eng.wait_ge(sem, value)


def build(nc, x, wq, wk, wv, bq, bk, bv, rw, wgu, wdn, wsg, wsu, wsd, out):
    ctx = ExitStack()
    with ctx:
        at = [16512]

        def sb(name, shape, dt=F32):
            n = 4
            for k in shape[1:]:
                n *= k
            t = nc.alloc_sbuf_tensor_at(name, shape, dt, offset=at[0])
            at[0] += (n + 31) // 32 * 32
            assert at[0] <= SBUF_END, (name, at[0])
            return t

        def sem(name):
            return ctx.enter_context(nc.semaphore(name))

        xn_d = nc.dram_tensor("xn_d", [T, D], F32, kind="Internal").ap()
        xs_d = nc.dram_tensor("xs_d", [SLOTS * P, D], F32, kind="Internal").ap()
        ys_d = nc.dram_tensor("ys_d", [SLOTS * P, D], F32, kind="Internal").ap()
        s_d = nc.dram_tensor("s_d", [T, D], F32, kind="Internal").ap()
        qk_d = nc.dram_tensor("qk_d", [UNITS, 2, 2, P, N], F32, kind="Internal").ap()

        ident = sb("ident", [P, P])
        score = sb("score", [P, TT])
        dest = sb("dest", [P, TT], I32)
        eid = sb("eid", [1, SLOTS + 1], I32)
        late_at = at[0]
        late = sb("late", [P, 3 * 1024])
        SG = late[:, 0:KD * 2 * F].rearrange("p (k f) -> p k f", k=KD)
        SD = late[:, KD * 2 * F:].rearrange("p (k f) -> p k f", k=KF)
        PT = late[:, 0:2048].rearrange("p (k c) -> p k c", k=2)
        xst = late[:, 2048:3072].rearrange("p (s j c) -> p s j c", s=2, j=2)
        wg_at = at[0]
        WG = sb("WG", [P, E, KD, 2 * F])
        WD = sb("WD", [P, E, KF, D])
        stage_at = at[0]

        at[0] = wg_at
        x_all = sb("x_all", [P, TT, D])
        xnr = sb("xnr", [P, GT, D])
        xT0 = sb("xT0", [P, 4, KD, P])
        zero = sb("zero", [P, ZT, D])
        stats = sb("stats", [P, TT, 6])
        mv = sb("mv", [P, TT, 2])
        mean = sb("mean", [P, TT])
        var = sb("var", [P, TT])
        root = sb("root", [P, TT])
        rstd = sb("rstd", [P, TT])
        tmp = sb("tmp", [P, TT])
        lg = sb("lg", [P, TT, E])
        oh = sb("oh", [P, TT, E])
        em8 = sb("em8", [P, TT, E])
        cand = sb("cand", [P, TT, E])
        incl = sb("incl", [P, TT, E])
        em8i = sb("em8i", [P, TT, E], I32)
        steps_i = sb("steps_i", [P, E, TT], I32)
        steps = sb("steps", [P, E, TT])
        slot_i = sb("slot_i", [P, SLOTS + 1, E], I32)
        slot_f = sb("slot_f", [P, SLOTS + 1, E])
        before = sb("before", [P, P])
        ones = sb("ones", [P, P])
        nt = sb("nt", [P, E])
        tend = sb("tend", [P, E])
        base = sb("base", [P, E])
        destf = sb("destf", [P, TT])
        eidf = sb("eidf", [P, SLOTS + 1])
        assert at[0] <= stage_at

        at[0] = stage_at
        QP = [sb(f"QP{w}", [P, UW], F32R) for w in range(RING)]
        KP = [sb(f"KP{w}", [P, UW], F32R) for w in range(RING)]
        stag = sb("stag", [P, 2, 2, N], F32R)
        xa = sb("xa", [P, 2, 2, D])
        xT = sb("xT", [P, 2, KD, N])
        V = sb("V", [P, 2, 2, H, 2 * DH])
        WQKV = sb("WQKV", [P, 3, KD, D])
        RW = sb("RW", [P, KD, E])
        bqk = sb("bqk", [P, 2, 2])
        bvb = sb("bvb", [P, D])
        OTs = sb("OTs", [P, 2, N])
        rden = sb("rden", [P, 16])
        sst = sb("sst", [P, 2, D])
        xr = sb("xr", [P, 2, D])
        idx2 = sb("idx2", [P, 2], I32)
        mx = sb("mx", [P, 2, UH, 2])
        mm = sb("mm", [16, 2, P], F32R)

        at[0] = stage_at
        xin = sb("xin", [P, 2, D])
        xTf = sb("xTf", [P, 2, KD, P])
        sgb = sb("sgb", [P, 2, F])
        hb = sb("hb", [P, 2, F])
        hTs = sb("hTs", [P, 2, KF, P])
        yb = sb("yb", [P, 2, D])
        rb = sb("rb", [P, 2, D])
        sl = sb("sl", [P, 2, D])
        xl = sb("xl", [P, 2, D])
        gz = sb("gz", [P, 2, D])
        o1 = sb("o1", [P, 2, D])
        ob = sb("ob", [P, 2, D])
        idx3 = sb("idx3", [P, 2], I32)

        ps = ctx.enter_context(nc.psum_tensor("ps", [P, 8, 512], F32))
        SA = [ps[:, a, :].rearrange("p (h k) -> p h k", k=N) for a in range(3)]
        PROJ, ST, PV, TRN = 3, 4, 6, 7
        SC = 8

        x_in = [sem(f"x_in{c}") for c in range(4)]
        const_in = sem("const_in")
        zero_set, zero_out = sem("zero_set"), sem("zero_out")
        pool_const, link, var_done, root_done = sem("pool_const"), sem("link"), sem("var_done"), sem("root_done")
        xn_ready, xn_out = sem("xn_ready"), [sem(f"xn_out{h}") for h in range(2)]
        tr_ready, tr_copied, lg_ready = sem("tr_ready"), sem("tr_copied"), sem("lg_ready")
        oh_ready, rank_ready, neg_max, exp_max, routed = (sem("oh_ready"), sem("rank_ready"), sem("neg_max"),
                                                          sem("exp_max"), sem("routed"))
        pads_set = sem("pads_set")
        xst_in, xa_in = [sem(f"xst_in{p}") for p in range(2)], [sem(f"xa_in{p}") for p in range(2)]
        xt_ready, xt_copied = sem("xt_ready"), sem("xt_copied")
        qk_ready, qk_hi, qk_lo = sem("qk_ready"), sem("qk_hi"), sem("qk_lo")
        qk_out = [sem(f"qk_out{w}") for w in range(RING)]
        packed = [sem(f"packed{w}") for w in range(RING)]
        v_ready, v_copied = sem("v_ready"), sem("v_copied")
        s_ready, s_reduced = sem("s_ready"), sem("s_reduced")
        mt_ready, m_hi, m_lo = sem("mt_ready"), sem("m_hi"), sem("m_lo")
        m_in = [sem(f"m_in{w}") for w in range(RING)]
        st_ready, exp_done, pv_done, o_copied = sem("st_ready"), sem("exp_done"), sem("pv_done"), sem("o_copied")
        ot_ready, inv_done, normed, s_added, s_out = (sem("ot_ready"), sem("inv_done"), sem("normed"), sem("s_added"),
                                                      sem("s_out"))
        xr_ready, scattered = sem("xr_ready"), [sem(f"scattered{j}") for j in range(2)]
        wg_in, sh_in = sem("wg_in"), sem("sh_in")
        xin_in = [sem(f"xin_in{p}") for p in range(2)]
        xf_ready, xf_copied = sem("xf_ready"), sem("xf_copied")
        gate_ready, up_ready, silu_done, h_done = sem("gate_ready"), sem("up_ready"), sem("silu_done"), sem("h_done")
        ht_ready, ht_copied, y_ready, y_copied = sem("ht_ready"), sem("ht_copied"), sem("y_ready"), sem("y_copied")
        y_out = [sem(f"y_out{p}") for p in range(2)]
        idx_set = sem("idx_set")
        batches_sent, tiles_fetched = sem("batches_sent"), sem("tiles_fetched")
        r_in, fin_in = [sem(f"r_in{p}") for p in range(2)], [sem(f"fin_in{p}") for p in range(2)]
        z_silu, gated, o_done = sem("z_silu"), sem("gated"), sem("o_done")
        o_out = [sem(f"o_out{p}") for p in range(2)]

        block = ctx.enter_context(nc.Block())

        def groups(eng, body):
            body(0)
            with eng.Fori(1, TT // GT) as i:
                body(i)

        def pairs(eng, body):
            body(0)
            with eng.Fori(1, PAIRS - 2) as i:
                body(i)
            body(PAIRS - 2)
            body(PAIRS - 1)

        def count(i, w, per=1, extra=0):
            return i * (RING * per) + (w * per + extra)

        def exists(i, w, ahead):
            return not isinstance(i, int) or RING * i + w + ahead < UNITS

        def slot_use(i, w):
            return w % RING, i + (w // RING + 1)

        FIRST_SHARED, TURNS = SLOTS, SLOTS + TT

        def turns(body):
            def kind(q):
                return "routed" if 0 <= q < FIRST_SHARED else "shared" if FIRST_SHARED <= q < TURNS else None

            def flat(q0, q1):
                for q in range(q0, q1):
                    body(q // 2, q % 2, kind(q), kind(q - 1), kind(q + 1), kind(q + 2))

            def loop(q0, q1):
                assert (q1 - q0) % 2 == 0
                same = (kind(q0),) * 4
                with body.engine.Fori(q0 // 2, q0 // 2 + (q1 - q0) // 2) as i:
                    body(i, q0 % 2, *same)
                    body(i + q0 % 2, 1 - q0 % 2, *same)
            flat(0, 3)
            loop(3, SLOTS - 2)
            flat(SLOTS - 2, SLOTS + 4)
            loop(SLOTS + 4, TURNS - 2)
            flat(TURNS - 2, TURNS + 1)

        def q_of(h, p):
            return h * 2 + p

        def before_turn(h, p):
            return (h, 0) if p else (h - 1, 1)

        def shared_use(h, p):
            return h - ((SLOTS + 1 - p) // 2 - 1)

        @block.sync
        def _(sp):
            xv = x.rearrange("(t p) c -> p t c", p=P)
            for c in range(4):
                sp.dma_start(x_all[:, 8 * c:8 * c + 8, :], xv[:, 8 * c:8 * c + 8, :]).then_inc(x_in[c], 16)
            for a, w in enumerate((wq, wk, wv)):
                sp.dma_start(WQKV[:, a, :, :], w.rearrange("(k p) c -> p k c", p=P)).then_inc(const_in, 16)
            sp.dma_start(RW[:, :, :], rw.rearrange("(k p) e -> p k e", p=P)).then_inc(const_in, 16)
            for a, w in enumerate((bq, bk)):
                sp.dma_start(bqk[:, a, :], w).then_inc(const_in, 16)
            sp.dma_start(bvb[:, :], bv.broadcast_to([P, D])).then_inc(const_in, 16)
            def store_xn(i):
                for hf in range(2):
                    sp.wait_ge(xn_ready, i * GT + (hf + 1) * GT // 2)
                    sp.dma_start(xn_d[bass.ds(i * (GT * P) + hf * P * GT // 2, P * GT // 2), :]
                                 .rearrange("(t p) c -> p t c", p=P),
                                 xnr[:, hf * GT // 2:(hf + 1) * GT // 2, :]).then_inc(xn_out[hf], 16)
            groups(sp, store_xn)
            for hf in range(2):
                sp.wait_ge(xn_out[hf], 16 * (TT // GT))

            def rows(b, parity, dst, done):
                sp.dma_start(dst[:, parity, :, :], xn_d[bass.ds(b * N, N), :].rearrange("(j p) c -> p j c", p=P))\
                  .then_inc(done[parity], 16)

            def store_qk(i, w):
                s, _ = slot_use(i, w)
                sp.wait_ge(qk_hi, count(i, w, 1, 1))
                sp.wait_ge(qk_lo, count(i, w, 1, 1))
                sp.dma_start(qk_d[bass.ds(count(i, w), 1), :, :, :, :].rearrange("u a l p t -> p (u a l) t"),
                             stag[:, :, :, :].rearrange("p a l t -> p (a l) t").bitcast(F32)).then_inc(qk_out[s], 16)

            def pack(i, w):
                s, use = slot_use(i, w)
                u, stored, used = count(i, w), use * 16, count(i, w, 4, -4 * (RING - 1))
                if not isinstance(i, int):
                    used, stored = sp.to_reg(used), sp.to_reg(stored)
                wait(sp, pv_done, used)
                sp.wait_ge(qk_out[s], stored)

                def part(a, l0, l1):
                    return qk_d[bass.ds(u, 1), a, l0:l1, :, :].rearrange("u l (d h) t -> (u l d) (h t)", h=UH)
                sp.dma_start(QP[s][0:2 * DH, :].bitcast(F32), part(0, 0, 2)).then_inc(packed[s], 16)
                sp.dma_start(QP[s][2 * DH:3 * DH, :].bitcast(F32), part(0, 0, 1)).then_inc(packed[s], 16)
                sp.dma_start(KP[s][0:DH, :].bitcast(F32), part(1, 0, 1)).then_inc(packed[s], 16)
                sp.dma_start(KP[s][DH:3 * DH, :].bitcast(F32), part(1, 0, 2)).then_inc(packed[s], 16)

            def max_rows(i, w):
                s, _ = slot_use(i, w)
                sp.wait_ge(m_hi, count(i, w, 1, 1))
                sp.wait_ge(m_lo, count(i, w, 1, 1))
                for l in range(2):
                    sp.dma_start(QP[s][MROW + l:MROW + l + 1, :].bitcast(F32).rearrange("o (r q) -> o r q", q=P),
                                 mm[:, l, :].bitcast(F32)).then_inc(m_in[s], 16)

            for b in range(2):
                rows(b, b, xst, xst_in)
            rows(0, 0, xa, xa_in)
            sp.wait_ge(pads_set, 2 * RING)
            sp.wait_ge(xt_ready, 1)
            rows(2, 0, xst, xst_in)
            for w in range(AHEAD):
                store_qk(0, w)
                if w < 3:
                    pack(0, w)
                if w == 2:
                    for s in range(SLOTS // ZT):
                        sp.dma_start(xs_d[s * ZT * P:(s + 1) * ZT * P, :].rearrange("(t p) c -> p t c", p=P),
                                     zero[:, :, :]).then_inc(zero_out, 16)
            max_rows(0, 0)

            def step(i, w):
                m, b = w % 2, i * 2 + w // 2
                if exists(i, w, 3):
                    pack(i, w + 3)
                if m == 0 and exists(i, w, 6):
                    sp.wait_ge(xt_ready, b + 2)
                    rows(b + 3, (w // 2 + 1) % 2, xst, xst_in)
                if exists(i, w, 1):
                    max_rows(i, w + 1)
                if m == 0:
                    wait(sp, s_added, count(i, w, 1, 0))
                    if not (isinstance(i, int) and RING * i + w == 0):
                        store_s(b - 1)
                    if exists(i, w, 2):
                        rows(b + 1, (w // 2 + 1) % 2, xa, xa_in)
                if exists(i, w, 5):
                    store_qk(i, w + 5)

            def store_s(b):
                sp.dma_start(s_d[bass.ds(b * N, N), :].rearrange("(j p) c -> p j c", p=P), sst[:, :, :])\
                  .then_inc(s_out, 16)

            def body(i):
                for w in range(RING):
                    step(i, w)
            pairs(sp, body)
            for j in range(2):
                sp.wait_ge(scattered[j], 16 * B)

            def load_in(h, p, kind):
                row = q_of(h, p) * P if kind == "routed" else q_of(h, p) * P - FIRST_SHARED * P
                src = xs_d if kind == "routed" else xn_d
                sp.dma_start(xin[:, p, :], src[bass.ds(row, P), :]).then_inc(xin_in[p], 16)

            sp.wait_ge(s_reduced, SC * UNITS)
            sp.wait_ge(pv_done, 4 * UNITS)
            load_in(0, 0, "routed")
            load_in(0, 1, "routed")
            sp.wait_ge(s_added, UNITS)
            store_s(B - 1)
            for h, w in enumerate((wsg, wsu)):
                sp.dma_start(SG[:, :, h * F:(h + 1) * F], w.rearrange("(k p) f -> p k f", p=P)).then_inc(sh_in, 16)
            sp.dma_start(SD[:, :, :], wsd.rearrange("(k p) c -> p k c", p=P)).then_inc(sh_in, 16)
            sp.wait_ge(s_out, 16 * B)

            def turn(h, p, kind, last, nxt, after):
                q, (h1, p1) = q_of(h, p), before_turn(h, p)
                if after:
                    sp.wait_ge(xf_ready, q + 1)
                    load_in(h + 1, p, after)
                if kind == "shared":
                    row = q * P - FIRST_SHARED * P
                    wait(sp, o_done, q - (FIRST_SHARED + 1))
                    sp.dma_start(sl[:, p, :], s_d[bass.ds(row, P), :]).then_inc(fin_in[p], 16)
                    sp.dma_start(xl[:, p, :], x[bass.ds(row, P), :]).then_inc(fin_in[p], 16)
                if last == "routed":
                    sp.wait_ge(y_copied, q)
                    sp.dma_start(ys_d[bass.ds(q * P - P, P), :], yb[:, p1, :]).then_inc(y_out[p1], 16)
                if last == "shared":
                    sp.wait_ge(o_done, q - FIRST_SHARED)
                    sp.dma_start(out[bass.ds(q * P - (1 + FIRST_SHARED) * P, P), :], ob[:, p1, :])\
                      .then_inc(o_out[p1], 16)
            turn.engine = sp
            turns(turn)
            for p in range(2):
                sp.wait_ge(o_out[p], 16 * TT // 2)

        @block.gpsimd
        def _(pool):
            g = nc.gpsimd
            g.memset(zero[:, :, :], 0.0).then_inc(zero_set, 1)
            g.memset(ident[:, :], 0.0).then_inc(pool_const, 1)
            g.memset(before[:, :], 1.0).then_inc(pool_const, 1)
            g.memset(ones[:, :], 1.0).then_inc(pool_const, 1)
            g.iota(em8i[:, :, :], pattern=[[0, TT], [1, E]], base=-E, channel_multiplier=0).then_inc(pool_const, 1)
            g.iota(steps_i[:, :, :], pattern=[[0, E], [P, TT]], base=0, channel_multiplier=0).then_inc(pool_const, 1)
            g.iota(slot_i[:, :, :], pattern=[[1, SLOTS + 1], [0, E]], base=0, channel_multiplier=0)\
             .then_inc(pool_const, 1)
            pool.wait_ge(pool_const, 6)
            g.affine_select(out=ident[:, :], in_=ident[:, :], compare_op=ALU.not_equal, fill=1.0, base=0,
                            pattern=[[-1, P]], channel_multiplier=1).then_inc(pool_const, 1)
            g.affine_select(out=before[:, :], in_=before[:, :], compare_op=ALU.is_gt, fill=0.0, base=0,
                            pattern=[[1, P]], channel_multiplier=-1).then_inc(pool_const, 1)
            g.memset(V[:, :, :, :, DH:].rearrange("p a b h c -> p (a b h) c"), 0.0)
            for w in range(RING):
                g.memset(QP[w][:, :].bitcast(F32), 0.0).then_inc(pads_set, 1)
                g.memset(KP[w][:, :].bitcast(F32), 0.0).then_inc(pads_set, 1)
            pool.wait_ge(pads_set, 2 * RING)
            g.memset(V[:, :, :, :, DH:DH + 1].rearrange("p a b h c -> p (a b h) c"), 1.0).then_inc(pads_set, 1)
            pool.wait_ge(pads_set, 2 * RING + 1)
            for w in range(RING):
                g.memset(KP[w][MROW:MROW + 2, :].bitcast(F32), 1.0).then_inc(pads_set, 1)
            pool.wait_ge(pads_set, 3 * RING + 1)

            pool.wait_ge(routed, 1)
            for hf in range(2):
                pool.wait_ge(xn_out[hf], 16 * (TT // GT))
            pool.wait_ge(zero_out, 16 * SLOTS // ZT)

            def load_expert(e, w):
                s, use = slot_use(e, w + 1)
                pool.wait_ge(m_in[s], use * 32)
                if w < KD:
                    pool.dma_start(WG[:, bass.ds(e, 1), w, :],
                                   wgu[bass.ds(e, 1), w * P:(w + 1) * P, :].rearrange("o p f -> p (o f)"))\
                        .then_inc(wg_in, 16)
                elif w == KD:
                    pool.dma_start(WD[:, bass.ds(e, 1), :, :],
                                   wdn[bass.ds(e, 1)].rearrange("o (k p) c -> p (o k) c", p=P)).then_inc(wg_in, 16)

            def scatter(i, w):
                b, par = i * 2 + w // 2, (w // 2) % 2
                pool.wait_ge(xa_in[par], i * 16 + 16)
                for j in range(2):
                    wait(pool, scattered[j], b * 16)
                    g.tensor_copy(idx2[:, j:j + 1], dest[:, bass.ds(b * 2 + j, 1)]).then_inc(xr_ready, 1)
                    g.tensor_tensor(xr[:, j, :], xa[:, par, j, :],
                                    score[:, bass.ds(b * 2 + j, 1)].to_broadcast([P, D]), ALU.mult).then_inc(xr_ready, 1)
                pool.wait_ge(xr_ready, b * 4 + 4)
                pool.sem_inc(batches_sent, 1)
                for j in range(2):
                    g.indirect_dma_start(out=xs_d, out_offset=bass.IndirectOffsetOnAxis(ap=idx2[:, j:j + 1], axis=0),
                                         in_=xr[:, j, :], in_offset=None).then_inc(scattered[j], 16)

            def add_xn(i, w):
                m, par = w % 2, (w // 2) % 2
                pool.wait_ge(normed, count(i, w, 1, 1))
                cols = slice(P * m, P * m + P)
                g.tensor_tensor(sst[:, :, cols], sst[:, :, cols], xa[:, par, :, cols], ALU.add).then_inc(s_added, 1)

            def body(i):
                for w in range(RING):
                    if w % 2 == 0:
                        scatter(i, w)
                    if not (isinstance(i, int) and i == 0 and w == 0):
                        add_xn(i, w - 1)
                    if w <= KD:
                        load_expert(i, w)
            pairs(pool, body)
            add_xn(PAIRS, -1)

            def turn(h, p, kind, last, nxt, after):
                q, (h1, p1) = q_of(h, p), before_turn(h, p)
                if kind == "shared":
                    if isinstance(q, int) and q == FIRST_SHARED:
                        for k in range(2):
                            pool.wait_ge(y_out[k], 16 * ((SLOTS + 1 - k) // 2))
                    pool.wait_ge(y_copied, q - 1)
                    g.tensor_copy(idx3[:, p:p + 1], dest[:, bass.ds(q - FIRST_SHARED, 1)]).then_inc(idx_set, 1)
                    pool.wait_ge(idx_set, q - (FIRST_SHARED - 1))
                    pool.sem_inc(tiles_fetched, 1)
                    g.indirect_dma_start(out=rb[:, p, :], out_offset=None, in_=ys_d,
                                         in_offset=bass.IndirectOffsetOnAxis(ap=idx3[:, p:p + 1], axis=0))\
                     .then_inc(r_in[p], 16)
                if last == "shared":
                    use = shared_use(h1, p1)
                    pool.wait_ge(z_silu, q - FIRST_SHARED)
                    pool.wait_ge(fin_in[p1], use * 32)
                    g.tensor_tensor(o1[:, p1, :], gz[:, p1, :], sl[:, p1, :], ALU.mult).then_inc(gated, 1)
                    pool.wait_ge(gated, q - FIRST_SHARED)
                    wait(pool, o_out[p1], use * 16 - 16)
                    g.tensor_tensor(ob[:, p1, :], o1[:, p1, :], xl[:, p1, :], ALU.add).then_inc(o_done, 1)
            turn.engine = pool
            turns(turn)

        @block.scalar
        def _(act):
            a_ = nc.scalar
            act.wait_ge(var_done, 1)
            a_.activation(root[:, :], var[:, :], ACT.Sqrt).then_inc(root_done, 1)

            def copy_t(i):
                for j in range(GT):
                    act.wait_ge(tr_ready, i * GT + j + 1)
                    wait(act, lg_ready, i * GT + j - 3)
                    a_.activation(xT0[:, j % 4, :, :].rearrange("p k c -> p (k c)"), ps[:, j % 4, 0:N], ACT.Copy)\
                      .then_inc(tr_copied, 1)
            groups(act, copy_t)
            act.wait_ge(neg_max, 1)
            a_.activation(score[:, :], tmp[:, :], ACT.Exp, scale=-1.0).then_inc(exp_max, 1)

            def xt_copy(b, par):
                act.wait_ge(xt_ready, b + 1)
                a_.activation(xT[:, par, :, :].rearrange("p k c -> p (k c)"), ps[:, TRN, :], ACT.Copy)\
                  .then_inc(xt_copied, 1)

            def hi_parts(i, w):
                act.wait_ge(qk_ready, count(i, w, 1, 1))
                if not (isinstance(i, int) and RING * i + w == 0):
                    s, use = slot_use(i, w - 1) if w % RING else (RING - 1, i + w // RING)
                    act.wait_ge(qk_out[s], use * 16)
                for a in range(2):
                    ins = a_.activation(stag[:, a, 0, :], ps[:, PROJ, a * N:(a + 1) * N], ACT.Identity,
                                        bias=bqk[:, a, w % 2:w % 2 + 1])
                ins.then_inc(qk_hi, 1)

            def max_hi(i, w):
                act.wait_ge(mt_ready, count(i, w, 1, 1))
                if not (isinstance(i, int) and RING * i + w == 0):
                    s, use = slot_use(i, w - 1) if w % RING else (RING - 1, i + w // RING)
                    act.wait_ge(m_in[s], use * 32)
                a_.mul(mm[:, 0, :], ps[0:16, TRN, 0:P], -1.0).then_inc(m_hi, 1)

            act.wait_ge(const_in, 16 * 7)
            xt_copy(0, 0)
            hi_parts(0, 0)
            xt_copy(1, 1)
            hi_parts(0, 1)
            hi_parts(0, 2)
            hi_parts(0, 3)
            xt_copy(2, 0)
            hi_parts(0, 4)
            max_hi(0, 0)

            def exps(i, w, c):
                gr, kt, hp = c // 4, c // 2 % 2, c % 2
                act.wait_ge(st_ready, count(i, w, 8, c + 1))
                if hp == 0:
                    wait(act, pv_done, count(i, w, 4, 2 * gr + kt - 1))
                a_.activation(PT[:, kt, hp * 512:hp * 512 + 512], ps[:, ST + c % 2, :], ACT.Exp,
                              scale=DH ** -0.5).then_inc(exp_done, 1)

            def o_copy(i, w, gr):
                act.wait_ge(pv_done, count(i, w, 4, 2 * gr + 2))
                wait(act, ot_ready, count(i, w, 1, 0))
                a_.activation(OTs[:, gr, :], ps[:, PV, 0:N], ACT.Copy).then_inc(o_copied, 1)

            def step(i, w):
                for c in range(5):
                    exps(i, w, c)
                if exists(i, w, 1):
                    max_hi(i, w + 1)
                exps(i, w, 5)
                o_copy(i, w, 0)
                if w % 2 == 1 and exists(i, w, 5):
                    xt_copy(i * 2 + (w // 2 + 3), (w // 2 + 1) % 2)
                exps(i, w, 6)
                exps(i, w, 7)
                if exists(i, w, 5):
                    hi_parts(i, w + 5)
                o_copy(i, w, 1)

            def body(i):
                for w in range(RING):
                    step(i, w)
            pairs(act, body)

            def xf_copy(h, p):
                q = q_of(h, p)
                act.wait_ge(xf_ready, q + 1)
                wait(act, up_ready, q - 1)
                a_.activation(xTf[:, p, :, :].rearrange("p k c -> p (k c)"), ps[:, 5, 0:D], ACT.Copy)\
                  .then_inc(xf_copied, 1)
            xf_copy(0, 0)

            def turn(h, p, kind, last, nxt, after):
                q, (h1, p1) = q_of(h, p), before_turn(h, p)
                if kind:
                    act.wait_ge(gate_ready, q + 1)
                    wait(act, h_done, q - 1)
                    a_.activation(sgb[:, p, :], ps[:, 2 * p, :], ACT.Silu).then_inc(silu_done, 1)
                if nxt:
                    xf_copy(*((h, 1) if p == 0 else (h + 1, 0)))
                if last == "shared":
                    act.wait_ge(y_copied, q)
                    a_.activation(gz[:, p1, :], yb[:, p1, :], ACT.Silu).then_inc(z_silu, 1)
            turn.engine = act
            turns(turn)

        @block.vector
        def _(dve):
            v = nc.vector
            done = [0]

            def chain(ins):
                done[0] += 1
                ins.then_inc(link, 1)
                dve.wait_ge(link, done[0])

            for c in range(4):
                dve.wait_ge(x_in[c], 16)
                for t in range(8 * c, 8 * c + 8):
                    ins = v.bn_stats(stats[:, t, :], x_all[:, t, :])
            chain(ins)
            for t in range(TT):
                ins = v.bn_aggr(mv[:, t, :], stats[:, t, :])
            chain(ins)
            v.tensor_copy(mean[:, :], mv[:, :, 0])
            v.tensor_scalar(var[:, :], mv[:, :, 1], EPS, None, ALU.add).then_inc(var_done, 1)
            dve.wait_ge(root_done, 1)
            chain(v.reciprocal(rstd[:, :], root[:, :]))
            chain(v.tensor_tensor(tmp[:, :], rstd[:, :], rstd[:, :], ALU.mult))
            chain(v.tensor_tensor(tmp[:, :], tmp[:, :], var[:, :], ALU.mult))
            chain(v.tensor_scalar(tmp[:, :], tmp[:, :], -0.5, 1.5, ALU.mult, ALU.add))
            chain(v.tensor_tensor(rstd[:, :], rstd[:, :], tmp[:, :], ALU.mult))

            def normalise(i):
                for j in range(GT):
                    t = i * GT + j
                    wait(dve, tr_ready, t - (GT - 1))
                    if j % (GT // 2) == 0:
                        wait(dve, xn_out[2 * j // GT], i * 16)
                    v.tensor_scalar(xnr[:, j, :], x_all[:, bass.ds(t, 1), :], mean[:, bass.ds(t, 1)],
                                    rstd[:, bass.ds(t, 1)], ALU.subtract, ALU.mult).then_inc(xn_ready, 1)
            groups(dve, normalise)

            dve.wait_ge(pool_const, 8)
            v.tensor_copy(em8[:, :, :], em8i[:, :, :])
            v.tensor_copy(steps[:, :, :], steps_i[:, :, :])
            v.tensor_copy(slot_f[:, :, :], slot_i[:, :, :])
            dve.wait_ge(lg_ready, TT)
            chain(v.tensor_copy(lg[:, :, :].rearrange("p t e -> p (t e)"), ps[:, TRN, 0:TT * E]))
            chain(v.reduce_max(tmp[:, :], lg[:, :, :], AX.X))
            dve.sem_inc(neg_max, 1)
            chain(v.tensor_tensor(oh[:, :, :], lg[:, :, :], tmp[:, :].rearrange("p (t o) -> p t o", o=1)
                                  .to_broadcast([P, TT, E]), ALU.is_equal))
            chain(v.tensor_tensor(cand[:, :, :], oh[:, :, :], em8[:, :, :], ALU.mult))
            chain(v.tensor_reduce(mean[:, :], cand[:, :, :], AX.X, ALU.min))
            v.tensor_tensor(oh[:, :, :], em8[:, :, :], mean[:, :].rearrange("p (t o) -> p t o", o=1)
                            .to_broadcast([P, TT, E]), ALU.is_equal).then_inc(oh_ready, 1)
            dve.wait_ge(exp_max, 1)
            chain(v.tensor_scalar(score[:, :], score[:, :], 1.0, None, ALU.add))
            chain(v.reciprocal(score[:, :], score[:, :]))
            dve.wait_ge(rank_ready, 1)
            chain(v.tensor_copy(cand[:, :, :].rearrange("p t e -> p (t e)"), ps[:, ST + 1, 0:TT * E]))
            chain(v.memset(lg[:, :, 0], 1.0))
            for e in range(E):
                ins = v.tensor_tensor_scan(incl[:, :, e], lg[:, :, 0], cand[:, :, e], 0.0, ALU.mult, ALU.add)
            chain(ins)
            chain(v.tensor_tensor(steps[:, :, :], incl[:, TT - 1, :].rearrange("p (e o) -> p e o", o=1)
                                  .to_broadcast([P, E, TT]), steps[:, :, :], ALU.is_gt))
            chain(v.reduce_sum(nt[:, :], steps[:, :, :], AX.X))
            chain(v.tensor_tensor_scan(tend[:, :], lg[:, 0:E, 0], nt[:, :], 0.0, ALU.mult, ALU.add))
            chain(v.tensor_tensor(base[:, :], tend[:, :], nt[:, :], ALU.subtract))
            chain(v.tensor_scalar(base[:, :], base[:, :], float(P), None, ALU.mult))
            chain(v.tensor_tensor(incl[:, :, :], incl[:, :, :], cand[:, :, :], ALU.subtract))
            chain(v.tensor_tensor(incl[:, :, :], incl[:, :, :], base[:, :].rearrange("p (o e) -> p o e", o=1)
                                  .to_broadcast([P, TT, E]), ALU.add))
            chain(v.tensor_tensor(incl[:, :, :].rearrange("p t e -> p (t e)"),
                                  incl[:, :, :].rearrange("p t e -> p (t e)"), ps[:, ST, 0:TT * E], ALU.add))
            chain(v.tensor_tensor(incl[:, :, :], incl[:, :, :], oh[:, :, :], ALU.mult))
            chain(v.reduce_sum(destf[:, :], incl[:, :, :], AX.X))
            chain(v.tensor_copy(dest[:, :], destf[:, :]))
            chain(v.tensor_tensor(slot_f[:, :, :], slot_f[:, :, :], tend[:, :].rearrange("p (o e) -> p o e", o=1)
                                  .to_broadcast([P, SLOTS + 1, E]), ALU.is_ge))
            chain(v.reduce_sum(eidf[:, :], slot_f[:, :, :], AX.X))
            chain(v.tensor_scalar(eidf[:, :], eidf[:, :], float(E - 1), None, ALU.min))
            v.tensor_copy(eid[0:1, :], eidf[0:1, :]).then_inc(routed, 1)

            def lo_parts(i, w):
                dve.wait_ge(qk_hi, count(i, w, 1, 1))
                for a in range(2):
                    ins = v.scalar_tensor_tensor(stag[:, a, 1, :], ps[:, PROJ, a * N:(a + 1) * N],
                                                 bqk[:, a, w % 2:w % 2 + 1], stag[:, a, 0, :].bitcast(F32),
                                                 ALU.add, ALU.subtract)
                ins.then_inc(qk_lo, 1)

            def v_copy(n_done, par, j):
                dve.wait_ge(v_ready, n_done)
                v.tensor_tensor(V[:, par, j, :, 0:DH], ps[:, PROJ, 0:D].rearrange("p (h d) -> p h d", d=DH),
                                bvb[:, :].rearrange("p (h d) -> p h d", d=DH), ALU.add).then_inc(v_copied, 1)

            def reduce_chunk(i, w, c):
                j, hp = c // 4, c % 4
                dve.wait_ge(s_ready, count(i, w, SC, c + 1))
                v.reduce_max(mx[:, w % 2, 2 * hp:2 * hp + 2, j], SA[c % 3], AX.X).then_inc(s_reduced, 1)

            def max_lo(i, w):
                dve.wait_ge(m_hi, count(i, w, 1, 1))
                v.scalar_tensor_tensor(mm[:, 1, :], ps[0:16, TRN, 0:P], -1.0, mm[:, 0, :].bitcast(F32),
                                       ALU.mult, ALU.subtract).then_inc(m_lo, 1)

            def norm(i, w):
                dve.wait_ge(ot_ready, count(i, w, 1, 1))
                o = ps[:, TRN, :].rearrange("p (g j h c) -> p g j h c", g=2, j=2, h=4)
                v.reciprocal(rden[:, :], ps[:, TRN, :].rearrange("p (r c) -> p r c", c=2 * DH)[:, :, DH])\
                 .then_inc(inv_done, 1)
                dve.wait_ge(inv_done, count(i, w, 1, 1))
                if w % 2 == 0:
                    wait(dve, s_out, (i * 2 + w // 2) * 16)
                inv = rden[:, :].rearrange("p (g j h o) -> p g j h o", g=2, j=2, h=4)
                for gr in range(2):
                    col = P * (w % 2) + 4 * DH * gr
                    ins = v.tensor_tensor(sst[:, :, col:col + 4 * DH].rearrange("p j (h d) -> p j h d", d=DH),
                                          o[:, gr, :, :, 0:DH], inv[:, gr, :, :, :].to_broadcast([P, 2, 4, DH]), ALU.mult)
                ins.then_inc(normed, 1)

            for w in range(4):
                lo_parts(0, w)
            dve.wait_ge(pads_set, 3 * RING + 1)
            v_copy(1, 0, 0)
            v_copy(2, 0, 1)
            lo_parts(0, 4)
            for c in range(SC):
                reduce_chunk(0, 0, c)
            max_lo(0, 0)
            for c in range(SC):
                reduce_chunk(0, 1, c)

            def step(i, w):
                first = isinstance(i, int) and RING * i + w == 0

                def ahead(c):
                    if exists(i, w, 2):
                        reduce_chunk(i, w + 2, c)
                ahead(0)
                if not first:
                    norm(i, w - 1)
                ahead(1)
                ahead(2)
                ahead(3)
                if exists(i, w, 1):
                    max_lo(i, w + 1)
                ahead(4)
                ahead(5)
                if exists(i, w, 2):
                    v_copy(count(i, w, 1, 3), (w // 2 + 1) % 2, w % 2)
                ahead(6)
                ahead(7)
                if exists(i, w, 5):
                    lo_parts(i, w + 5)

            def body(i):
                for w in range(RING):
                    step(i, w)
            pairs(dve, body)
            norm(PAIRS, -1)

            def turn(h, p, kind, last, nxt, after):
                q, (h1, p1) = q_of(h, p), before_turn(h, p)
                if last:
                    dve.wait_ge(ht_ready, q)
                    wait(dve, y_ready, q - 2)
                    v.tensor_copy(hTs[:, p1, :, :].rearrange("p k c -> p (k c)"), ps[:, 4, :]).then_inc(ht_copied, 1)
                if kind:
                    dve.wait_ge(silu_done, q + 1)
                    dve.wait_ge(up_ready, q + 1)
                    wait(dve, ht_ready, q - 1)
                    v.tensor_tensor(hb[:, p, :], sgb[:, p, :], ps[:, 2 * p + 1, :], ALU.mult).then_inc(h_done, 1)
                if last:
                    dve.wait_ge(y_ready, q)
                    y = ps[:, 6 + p1, 0:D]
                    if last == "routed":
                        wait(dve, y_out[p1], h1 * 16)
                        v.tensor_copy(yb[:, p1, :], y).then_inc(y_copied, 1)
                    else:
                        if isinstance(q, int) and q <= FIRST_SHARED + 2:
                            for k in range(2):
                                dve.wait_ge(y_out[k], 16 * ((SLOTS + 1 - k) // 2))
                        wait(dve, z_silu, q - (FIRST_SHARED + 2))
                        dve.wait_ge(r_in[p1], shared_use(h1, p1) * 16)
                        v.tensor_tensor(yb[:, p1, :], y, rb[:, p1, :], ALU.add).then_inc(y_copied, 1)
            turn.engine = dve
            turns(turn)

        @block.tensor
        def _(pe):
            mmul = nc.tensor.matmul
            pe.wait_ge(pool_const, 8)
            pe.wait_ge(const_in, 16 * 7)

            def transpose(dst, src):
                return nc.tensor.transpose(dst, src, ident[:, :])

            def logits(i):
                def tr(j):
                    pe.wait_ge(xn_ready, i * GT + j + 1)
                    wait(pe, tr_copied, i * GT + j - 3)
                    for k in range(KD):
                        ins = transpose(ps[:, j % 4, k * P:(k + 1) * P], xnr[:, j, k * P:(k + 1) * P])
                    ins.then_inc(tr_ready, 1)

                def lo(j):
                    pe.wait_ge(tr_copied, i * GT + j + 1)
                    for k in range(KD):
                        ins = mmul(ps[:, TRN, bass.ds((i * GT + j) * E, E)], xT0[:, j % 4, k, :], RW[:, k, :],
                                   start=(k == 0), stop=(k == KD - 1))
                    ins.then_inc(lg_ready, 1)
                tr(0)
                tr(1)
                for j in range(2, GT):
                    tr(j)
                    lo(j - 2)
                lo(GT - 2)
                lo(GT - 1)
            groups(pe, logits)
            pe.wait_ge(oh_ready, 1)
            hot = oh[:, :, :].rearrange("p t e -> p (t e)")
            mmul(ps[:, ST, 0:TT * E], before[:, :], hot, start=True, stop=True)
            mmul(ps[:, ST + 1, 0:TT * E], ones[:, :], hot, start=True, stop=True).then_inc(rank_ready, 1)
            pe.wait_ge(routed, 1)

            def xt(b, par, nth):
                pe.wait_ge(xst_in[par], nth * 16)
                for j in range(2):
                    for k in range(KD):
                        ins = transpose(ps[:, TRN, k * N + j * P:k * N + (j + 1) * P],
                                        xst[:, par, j, k * P:(k + 1) * P])
                ins.then_inc(xt_ready, 1)

            def qk(w, par):
                for a in range(2):
                    for k in range(KD):
                        ins = mmul(ps[:, PROJ, a * N:(a + 1) * N], WQKV[:, a, k, w % 2 * P:(w % 2 + 1) * P],
                                   xT[:, par, k, :], start=(k == 0), stop=(k == KD - 1))
                ins.then_inc(qk_ready, 1)

            def v_tile(par, j):
                for k in range(KD):
                    ins = mmul(ps[:, PROJ, 0:D], xT[:, par, k, j * P:(j + 1) * P], WQKV[:, 2, k, :],
                               start=(k == 0), stop=(k == KD - 1))
                ins.then_inc(v_ready, 1)

            def scores(i, w, c):
                s, use = slot_use(i, w)
                j, hp = c // 4, c % 4
                if c == 0:
                    pe.wait_ge(packed[s], use * 64)
                wait(pe, s_reduced, count(i, w, SC, (-1, 0, -2)[c] if c < 3 else c - 2))
                for h in range(2):
                    col = (2 * hp + h) * N
                    ins = mmul(SA[c % 3][:, h, :], QP[s][0:SPLIT_ROWS, col + j * P:col + (j + 1) * P],
                               KP[s][0:SPLIT_ROWS, col:col + N], start=True, stop=True)
                ins.then_inc(s_ready, 1)

            def max_t(i, w):
                pe.wait_ge(s_reduced, count(i, w, SC, SC))
                transpose(ps[0:16, TRN, 0:P], mx[:, w % 2, :, :].rearrange("p h j -> p (h j)")).then_inc(mt_ready, 1)

            def scores_t(i, w, c):
                s, use = slot_use(i, w)
                gr, kt, hp = c // 4, c // 2 % 2, c % 2
                if c == 0:
                    pe.wait_ge(m_in[s], use * 32)
                wait(pe, exp_done, count(i, w, 8, c - 1))
                for h in range(2):
                    col = (4 * gr + 2 * hp + h) * N
                    ins = mmul(ps[:, ST + c % 2, h * N:(h + 1) * N], KP[s][:, col + kt * P:col + (kt + 1) * P],
                               QP[s][:, col:col + N], start=True, stop=True)
                ins.then_inc(st_ready, 1)

            def weighted(i, w, gr, kt):
                pe.wait_ge(exp_done, count(i, w, 8, 4 * gr + 2 * kt + 2))
                if kt == 0:
                    wait(pe, o_copied, count(i, w, 2, gr))
                for h in range(4):
                    head = UH * (w % 2) + 4 * gr + h
                    ins = mmul(ps[32 * h:32 * h + 32, PV, 0:N], V[:, (w // 2) % 2, kt, head, :],
                               PT[:, kt, h * N:(h + 1) * N], start=(kt == 0), stop=(kt == 1),
                               tile_position=(0, 32 * h))
                ins.then_inc(pv_done, 1)

            def out_t(i, w):
                pe.wait_ge(o_copied, count(i, w, 2, 2))
                for gr in range(2):
                    for j in range(2):
                        c = (2 * gr + j) * P
                        ins = transpose(ps[:, TRN, c:c + P], OTs[:, gr, j * P:(j + 1) * P])
                ins.then_inc(ot_ready, 1)

            xt(0, 0, 1)
            pe.wait_ge(xt_copied, 1)
            qk(0, 0)
            xt(1, 1, 1)
            pe.wait_ge(qk_lo, 1)
            qk(1, 0)
            pe.wait_ge(xt_copied, 2)
            pe.wait_ge(qk_lo, 2)
            qk(2, 1)
            pe.wait_ge(qk_lo, 3)
            qk(3, 1)
            pe.wait_ge(qk_lo, 4)
            v_tile(0, 0)
            pe.wait_ge(v_copied, 1)
            v_tile(0, 1)
            xt(2, 0, 2)
            pe.wait_ge(v_copied, 2)
            pe.wait_ge(xt_copied, 3)
            qk(4, 0)
            for c in range(SC):
                scores(0, 0, c)
            max_t(0, 0)
            for c in range(SC):
                scores(0, 1, c)

            def step(i, w):
                m, par = w % 2, w // 2
                first = isinstance(i, int) and RING * i + w == 0

                def ahead(c):
                    if exists(i, w, 2):
                        scores(i, w + 2, c)
                scores_t(i, w, 0)
                ahead(0)
                scores_t(i, w, 1)
                ahead(1)
                if not first:
                    pe.wait_ge(m_lo, count(i, w, 1, 1))
                    out_t(i, w - 1)
                scores_t(i, w, 2)
                ahead(2)
                scores_t(i, w, 3)
                weighted(i, w, 0, 0)
                ahead(3)
                scores_t(i, w, 4)
                if exists(i, w, 1):
                    if first:
                        pe.wait_ge(m_lo, 1)
                    else:
                        pe.wait_ge(normed, count(i, w, 1, 0))
                    max_t(i, w + 1)
                ahead(4)
                scores_t(i, w, 5)
                weighted(i, w, 0, 1)
                ahead(5)
                if exists(i, w, 2):
                    if exists(i, w, 4):
                        pe.wait_ge(qk_lo, count(i, w, 1, 5))
                    else:
                        pe.wait_ge(v_copied, count(i, w, 1, 2))
                    v_tile(1 - par, m)
                if m == 1 and exists(i, w, 5):
                    pe.wait_ge(m_lo, count(i, w, 1, 2))
                    xt(None, 1 - par, i + 2 + par)
                scores_t(i, w, 6)
                ahead(6)
                scores_t(i, w, 7)
                weighted(i, w, 1, 0)
                ahead(7)
                if exists(i, w, 5):
                    pe.wait_ge(v_copied, count(i, w, 1, 3))
                    if m == 1:
                        pe.wait_ge(xt_copied, i * 2 + (par + 4))
                    qk(w + 5, par if m == 0 else 1 - par)
                weighted(i, w, 1, 1)

            def body(i):
                for w in range(RING):
                    step(i, w)
            pairs(pe, body)
            pe.wait_ge(normed, UNITS - 1)
            out_t(PAIRS, -1)

            def xf(h, p):
                q = q_of(h, p)
                pe.wait_ge(xin_in[p], h * 16 + 16)
                wait(pe, xf_copied, q)
                for k in range(KD):
                    ins = transpose(ps[:, 5, k * P:(k + 1) * P], xin[:, p, k * P:(k + 1) * P])
                ins.then_inc(xf_ready, 1)

            pe.wait_ge(exp_done, 8 * UNITS)
            xf(0, 0)
            pe.wait_ge(wg_in, (KD + 1) * 16 * E)
            pe.wait_ge(s_reduced, SC * UNITS)
            pe.wait_ge(normed, UNITS)

            def turn(h, p, kind, last, nxt, after):
                q, (h1, p1) = q_of(h, p), before_turn(h, p)

                def gate_up(half, done):
                    for k in range(KD):
                        ws = SG[:, k, half * F:(half + 1) * F] if kind == "shared" else \
                            WG[:, bass.ds(e_now, 1), k, half * F:(half + 1) * F]
                        ins = mmul(ps[:, 2 * p + half, :], xTf[:, p, k, :], ws, start=(k == 0), stop=(k == KD - 1))
                    ins.then_inc(done, 1)
                if kind == "shared" and isinstance(q, int) and q == FIRST_SHARED:
                    pe.wait_ge(sh_in, 3 * 16)
                if kind:
                    if kind == "routed":
                        e_now = pe.value_load(eid[0:1, bass.ds(q, 1)], min_val=0, max_val=E - 1)
                    pe.wait_ge(xf_copied, q + 1)
                    wait(pe, silu_done, q - 1)
                    gate_up(0, gate_ready)
                if last:
                    pe.wait_ge(h_done, q)
                    wait(pe, ht_copied, q - 1)
                    for k in range(KF):
                        ins = transpose(ps[:, 4, k * P:(k + 1) * P], hb[:, p1, k * P:(k + 1) * P])
                    ins.then_inc(ht_ready, 1)
                if kind:
                    wait(pe, h_done, q - 1)
                    gate_up(1, up_ready)
                if nxt:
                    xf(*((h, 1) if p == 0 else (h + 1, 0)))
                if last:
                    if last == "routed":
                        e_last = pe.value_load(eid[0:1, bass.ds(q - 1, 1)], min_val=0, max_val=E - 1)
                    pe.wait_ge(ht_copied, q)
                    wait(pe, y_copied, q - 2)
                    for k in range(KF):
                        ws = SD[:, k, :] if last == "shared" else WD[:, bass.ds(e_last, 1), k, :]
                        ins = mmul(ps[:, 6 + p1, 0:D], hTs[:, p1, k, :], ws, start=(k == 0), stop=(k == KF - 1))
                    ins.then_inc(y_ready, 1)
            turn.engine = pe
            turns(turn)


def kernel(**inputs):
    import numpy as np
    import concourse.bacc as bacc
    from concourse.bass_utils import run_bass_kernel_spmd

    a = {k[3:]: np.asarray(v) for k, v in inputs.items()}

    def by_dim(w):
        return np.ascontiguousarray(w.reshape(w.shape[:-1] + (2, UH, DH)).swapaxes(-1, -2).reshape(w.shape))

    arrays = {
        "x": a["attn_x"].reshape(T, D),
        "wq": by_dim(a["attn_Wq"]), "wk": by_dim(a["attn_Wk"]), "wv": a["attn_Wv"],
        "bq": by_dim(a["attn_bq"]).reshape(2, P).T, "bk": by_dim(a["attn_bk"]).reshape(2, P).T,
        "bv": a["attn_bv"].reshape(1, D), "rw": a["ffn_router_w"].T,
        "wgu": a["ffn_gate_up_proj"], "wdn": a["ffn_down_proj"],
        "wsg": a["ffn_shared_gate_w"], "wsu": a["ffn_shared_up_w"], "wsd": a["ffn_shared_down_w"],
    }
    nc = bacc.Bacc("TRN2", target_bir_lowering=False, num_devices=1)
    maps, args = {}, []
    for name, v in arrays.items():
        v = np.ascontiguousarray(v)
        maps["in_" + name] = v
        args.append(nc.dram_tensor("in_" + name, v.shape, F32, kind="ExternalInput").ap())
    args.append(nc.dram_tensor("out", (T, D), F32, kind="ExternalOutput").ap())
    build(nc, *args)
    r = run_bass_kernel_spmd(nc, [maps], core_ids=[0])
    return r.results[0]["out"].reshape(B, N, D)
```

```python
from contextlib import ExitStack

import concourse.bass as bass
from concourse import mybir

F32, F32R, I32 = mybir.dt.float32, mybir.dt.float32r, mybir.dt.int32
ACT = mybir.ActivationFunctionType
ALU = mybir.AluOpType
AX = mybir.AxisListType

P = 128
B, N, D, H = 16, 256, 256, 16
DH = D // H
T = B * N
TT = T // P
KD = D // P
E, F = 8, 512
KF = F // P
SLOTS = TT + E - 1
UH = 8
UNITS = B * H // UH
UW = UH * N
RING = 4
EPS = 1e-5
SPLIT_ROWS = 3 * DH
MROW = 64
PAIRS = B // 2
PADS = SLOTS - TT
EC = 32
AHEAD = 5
WH = KD * 2 * F // 2 + KF * D // 2
WRING = 3
SPLITS = 4
GT = 8
SBUF_END = 229344


def wait(eng, sem, value):
    if not isinstance(value, int) or value > 0:
        eng.wait_ge(sem, value)


def build(nc, x, wq, wk, wv, bq, bk, bv, rw, wgu, wdn, wsg, wsu, wsd, out):
    ctx = ExitStack()
    with ctx:
        at = [16512]

        def sb(name, shape, dt=F32):
            n = 4
            for k in shape[1:]:
                n *= k
            t = nc.alloc_sbuf_tensor_at(name, shape, dt, offset=at[0])
            at[0] += (n + 31) // 32 * 32
            assert at[0] <= SBUF_END, (name, at[0])
            return t

        def sem(name):
            return ctx.enter_context(nc.semaphore(name))

        xn_d = nc.dram_tensor("xn_d", [T, D], F32, kind="Internal").ap()
        xs_d = nc.dram_tensor("xs_d", [SLOTS * P, D], F32, kind="Internal").ap()
        ys_d = nc.dram_tensor("ys_d", [SLOTS * P, D], F32, kind="Internal").ap()
        s_d = nc.dram_tensor("s_d", [T, D], F32, kind="Internal").ap()
        qk_d = nc.dram_tensor("qk_d", [UNITS, 2, 2, P, N], F32, kind="Internal").ap()

        ident = sb("ident", [P, P])
        score = sb("score", [P, TT])
        dest = sb("dest", [P, TT], I32)
        pad_row = sb("pad_row", [P, PADS], I32)
        zero = sb("zero", [P, D])
        half_at = sb("half_at", [1, SLOTS + 1], I32)
        splits_by = sb("splits_by", [1, SLOTS + 1], I32)
        slots_by = sb("slots_by", [1, E], I32)
        late_at = at[0]
        late = sb("late", [P, 3 * 1024])
        SRAW = late[:, :].rearrange("p (h c) -> p h c", h=2)
        at[0] = late_at
        SLO = sb("SLO", [P, 2, WH], F32R)
        PT = late[:, 0:2048].rearrange("p (k c) -> p k c", k=2)
        xst = late[:, 2048:3072].rearrange("p (s j c) -> p s j c", s=2, j=2)
        wg_at = at[0]
        WRAW = sb("WRAW", [P, 2 * WRING, WH])
        at[0] = wg_at
        WLO = sb("WLO", [P, 2 * WRING, WH], F32R)
        WHI = sb("WHI", [P, 2 * WRING, WH], F32R)
        stage_at = at[0]

        at[0] = wg_at
        x_all = sb("x_all", [P, TT, D])
        xnr = sb("xnr", [P, GT, D])
        xT0 = sb("xT0", [P, 2, KD, 4 * P])
        lT = sb("lT", [P, 2, P])
        stats = sb("stats", [P, TT, 6])
        mv = sb("mv", [P, TT, 2])
        mean = sb("mean", [P, TT])
        var = sb("var", [P, TT])
        root = sb("root", [P, TT])
        rstd = sb("rstd", [P, TT])
        tmp = sb("tmp", [P, TT])
        lg = sb("lg", [P, TT, E])
        oh = sb("oh", [P, TT, E])
        em8 = sb("em8", [P, TT, E])
        cand = sb("cand", [P, TT, E])
        incl = sb("incl", [P, TT, E])
        rank = sb("rank", [P, TT, E])
        em8i = sb("em8i", [P, TT, E], I32)
        steps_i = sb("steps_i", [P, E, TT], I32)
        steps = sb("steps", [P, E, TT])
        slot_i = sb("slot_i", [P, SLOTS + 1, E], I32)
        slot_f = sb("slot_f", [P, SLOTS + 1, E])
        pad_i = sb("pad_i", [P, PADS, E], I32)
        pad_f = sb("pad_f", [P, PADS, E])
        pad_c = sb("pad_c", [P, PADS, E])
        pad_s = sb("pad_s", [P, PADS])
        cnt = sb("cnt", [P, E])
        free = sb("free", [P, E])
        before = sb("before", [P, P])
        ones = sb("ones", [P, P])
        nt = sb("nt", [P, E])
        tend = sb("tend", [P, E])
        base = sb("base", [P, E])
        destf = sb("destf", [P, TT])
        eidf = sb("eidf", [P, SLOTS + 1])
        sel = sb("sel", [P, SLOTS + 1])
        cntf = sb("cntf", [P, SLOTS + 1])
        assert at[0] <= stage_at

        at[0] = stage_at
        QP = [sb(f"QP{w}", [P, UW], F32R) for w in range(RING)]
        KP = [sb(f"KP{w}", [P, UW], F32R) for w in range(RING)]
        stag = sb("stag", [P, 2, 2, N], F32R)
        xa = sb("xa", [P, 2, 2, D])
        xT = sb("xT", [P, 2, 2, KD, N], F32R)
        V = sb("V", [P, 2, 2, H, 2 * DH])
        wraw_at = at[0]
        W3RAW = sb("W3RAW", [P, 3, KD, D])
        at[0] = wraw_at
        W3LO = sb("W3LO", [P, 3, KD, D], F32R)
        W3HI = sb("W3HI", [P, 3, KD, D], F32R)
        W3 = (W3HI, W3LO)
        TERMS = ((0, 0), (0, 1), (1, 0))
        RW = sb("RW", [P, KD, EC])
        bqk = sb("bqk", [P, 2, 2])
        bvb = sb("bvb", [P, D])
        OTs = sb("OTs", [P, 2, N])
        rden = sb("rden", [P, 16])
        sst = sb("sst", [P, 2, D])
        xr = sb("xr", [P, 2, D])
        idx2 = sb("idx2", [P, 2], I32)
        idx_pad = sb("idx_pad", [P, 1], I32)
        mx = sb("mx", [P, 2, UH, 2])
        mm = sb("mm", [16, 2, P], F32R)

        xin = sb("xin", [P, 2, D])
        xTf = sb("xTf", [P, 2, 2, KD * P], F32R)
        at[0] = stage_at
        SHI = sb("SHI", [P, 2, WH], F32R)
        sgb = sb("sgb", [P, 2, F])
        hb = sb("hb", [P, 2, F])
        hTs = sb("hTs", [P, 2, 2, KF * P], F32R)
        yb = sb("yb", [P, 2, D])
        rb = sb("rb", [P, 2, D])
        sl = sb("sl", [P, 2, D])
        xl = sb("xl", [P, 2, D])
        gz = sb("gz", [P, 2, D])
        o1 = sb("o1", [P, 2, D])
        ob = sb("ob", [P, 2, D])
        idx3 = sb("idx3", [P, 2], I32)

        ps = ctx.enter_context(nc.psum_tensor("ps", [P, 8, 512], F32))
        SA = [ps[:, a, :].rearrange("p (h k) -> p h k", k=N) for a in range(3)]
        PROJ, ST, PV, TRN = 3, 4, 6, 7
        LT = (2, PV)
        SC = 8

        x_in = [sem(f"x_in{c}") for c in range(4)]
        const_in, rw_in = sem("const_in"), sem("rw_in")
        zero_set, zero_out = sem("zero_set"), sem("zero_out")
        pool_const, link, var_done, root_done = sem("pool_const"), sem("link"), sem("var_done"), sem("root_done")
        xn_ready, xn_out = sem("xn_ready"), [sem(f"xn_out{h}") for h in range(2)]
        tr_ready, tr_copied, lm_ready, lt_copied = sem("tr_ready"), sem("tr_copied"), sem("lm_ready"), sem("lt_copied")
        lg_ready, lg_copied, rw_set = sem("lg_ready"), sem("lg_copied"), sem("rw_set")
        oh_ready, rank_ready, rank_read, neg_max, exp_max, routed = (sem("oh_ready"), sem("rank_ready"), sem("rank_read"),
                                                                     sem("neg_max"),
                                                          sem("exp_max"), sem("routed"))
        pads_set = sem("pads_set")
        xst_in, xa_in = [sem(f"xst_in{p}") for p in range(2)], [sem(f"xa_in{p}") for p in range(2)]
        xt_ready, xt_hi, xt_lo, w3_hi, w3_split = sem("xt_ready"), sem("xt_hi"), sem("xt_lo"), sem("w3_hi"), sem("w3_split")
        qk_ready, qk_hi, qk_lo = sem("qk_ready"), sem("qk_hi"), sem("qk_lo")
        qk_out = [sem(f"qk_out{w}") for w in range(RING)]
        packed = [sem(f"packed{w}") for w in range(RING)]
        v_ready, v_copied = sem("v_ready"), sem("v_copied")
        s_ready, s_reduced = sem("s_ready"), sem("s_reduced")
        mt_ready, m_hi, m_lo = sem("mt_ready"), sem("m_hi"), sem("m_lo")
        m_in = [sem(f"m_in{w}") for w in range(RING)]
        st_ready, exp_done, pv_done, o_copied = sem("st_ready"), sem("exp_done"), sem("pv_done"), sem("o_copied")
        ot_ready, inv_done, normed, s_added, s_out = (sem("ot_ready"), sem("inv_done"), sem("normed"), sem("s_added"),
                                                      sem("s_out"))
        xr_ready, scattered = sem("xr_ready"), [sem(f"scattered{j}") for j in range(2)]
        late_in = [sem(f"late_in{h}") for h in range(2)]
        half_in, w_split, sh_in, sh_split = sem("half_in"), sem("w_split"), sem("sh_in"), sem("sh_split")
        pad_set, fills_sent = sem("pad_set"), sem("fills_sent")
        hi_set, splits_begun = sem("hi_set"), sem("splits_begun")
        xin_in = [sem(f"xin_in{p}") for p in range(2)]
        xf_ready, xf_hi, xf_lo = sem("xf_ready"), sem("xf_hi"), sem("xf_lo")
        gate_ready, up_ready, silu_done, h_done = sem("gate_ready"), sem("up_ready"), sem("silu_done"), sem("h_done")
        ht_ready, ht_hi, ht_lo = sem("ht_ready"), sem("ht_hi"), sem("ht_lo")
        y_ready, y_copied = sem("y_ready"), sem("y_copied")
        y_out = [sem(f"y_out{p}") for p in range(2)]
        idx_set = sem("idx_set")
        batches_sent, tiles_fetched = sem("batches_sent"), sem("tiles_fetched")
        r_in, fin_in = [sem(f"r_in{p}") for p in range(2)], [sem(f"fin_in{p}") for p in range(2)]
        z_silu, gated, o_done = sem("z_silu"), sem("gated"), sem("o_done")
        o_out = [sem(f"o_out{p}") for p in range(2)]

        assert PADS == PAIRS - 1

        block = ctx.enter_context(nc.Block())

        def pairs(eng, body):
            body(0)
            with eng.Fori(1, PAIRS - 2) as i:
                body(i)
            body(PAIRS - 2)
            body(PAIRS - 1)

        def count(i, w, per=1, extra=0):
            return i * (RING * per) + (w * per + extra)

        def exists(i, w, ahead):
            return not isinstance(i, int) or RING * i + w + ahead < UNITS

        def slot_use(i, w):
            return w % RING, i + (w // RING + 1)

        FIRST_SHARED, TURNS = SLOTS, SLOTS + TT

        def turns(body):
            def kind(q):
                return "routed" if 0 <= q < FIRST_SHARED else "shared" if FIRST_SHARED <= q < TURNS else None

            def flat(q0, q1):
                for q in range(q0, q1):
                    body(q // 2, q % 2, kind(q), kind(q - 1), kind(q + 1), kind(q + 2))

            def loop(q0, q1):
                assert (q1 - q0) % 2 == 0
                same = (kind(q0),) * 4
                with body.engine.Fori(q0 // 2, q0 // 2 + (q1 - q0) // 2) as i:
                    body(i, q0 % 2, *same)
                    body(i + q0 % 2, 1 - q0 % 2, *same)
            flat(0, 3)
            loop(3, SLOTS - 2)
            flat(SLOTS - 2, SLOTS + 4)
            loop(SLOTS + 4, TURNS - 2)
            flat(TURNS - 2, TURNS + 1)

        def q_of(h, p):
            return h * 2 + p

        def before_turn(h, p):
            return (h, 0) if p else (h - 1, 1)

        def shared_use(h, p):
            return h - ((SLOTS + 1 - p) // 2 - 1)

        @block.sync
        def _(sp):
            xv = x.rearrange("(t p) c -> p t c", p=P)
            def load_x(c):
                some = slice(c * GT, (c + 1) * GT)
                sp.dma_start(x_all[:, some, :], xv[:, some, :]).then_inc(x_in[c], 16)
            load_x(0)
            sp.wait_ge(rw_set, 1)
            sp.dma_start(RW[:, :, 0:E], rw.rearrange("(k p) e -> p k e", p=P)).then_inc(rw_in, 16)
            for c in range(1, TT // GT):
                load_x(c)
            for a, w in enumerate((wq, wk, wv)):
                sp.dma_start(W3RAW[:, a, :, :], w.rearrange("(k p) c -> p k c", p=P)).then_inc(const_in, 16)
            for a, w in enumerate((bq, bk)):
                sp.dma_start(bqk[:, a, :], w).then_inc(const_in, 16)
            sp.dma_start(bvb[:, :], bv.broadcast_to([P, D])).then_inc(const_in, 16)

            def store_xn(i):
                for hf in range(2):
                    sp.wait_ge(xn_ready, i * GT + (hf + 1) * GT // 2)
                    sp.dma_start(xn_d[bass.ds(i * (GT * P) + hf * P * GT // 2, P * GT // 2), :]
                                 .rearrange("(t p) c -> p t c", p=P),
                                 xnr[:, hf * GT // 2:(hf + 1) * GT // 2, :]).then_inc(xn_out[hf], 16)
            def rows(b, parity, dst, done):
                sp.dma_start(dst[:, parity, :, :], xn_d[bass.ds(b * N, N), :].rearrange("(j p) c -> p j c", p=P))\
                  .then_inc(done[parity], 16)

            def store_qk(i, w):
                s, _ = slot_use(i, w)
                sp.wait_ge(qk_hi, count(i, w, 1, 1))
                sp.wait_ge(qk_lo, count(i, w, 1, 1))
                sp.dma_start(qk_d[bass.ds(count(i, w), 1), :, :, :, :].rearrange("u a l p t -> p (u a l) t"),
                             stag[:, :, :, :].rearrange("p a l t -> p (a l) t").bitcast(F32)).then_inc(qk_out[s], 16)

            def pack(i, w):
                s, use = slot_use(i, w)
                u, stored, used = count(i, w), use * 16, count(i, w, 4, -4 * (RING - 1))
                if not isinstance(i, int):
                    used, stored = sp.to_reg(used), sp.to_reg(stored)
                wait(sp, pv_done, used)
                sp.wait_ge(qk_out[s], stored)

                def part(a, l0, l1):
                    return qk_d[bass.ds(u, 1), a, l0:l1, :, :].rearrange("u l (d h) t -> (u l d) (h t)", h=UH)
                sp.dma_start(QP[s][0:2 * DH, :].bitcast(F32), part(0, 0, 2)).then_inc(packed[s], 16)
                sp.dma_start(QP[s][2 * DH:3 * DH, :].bitcast(F32), part(0, 0, 1)).then_inc(packed[s], 16)
                sp.dma_start(KP[s][0:DH, :].bitcast(F32), part(1, 0, 1)).then_inc(packed[s], 16)
                sp.dma_start(KP[s][DH:3 * DH, :].bitcast(F32), part(1, 0, 2)).then_inc(packed[s], 16)

            def max_rows(i, w):
                s, _ = slot_use(i, w)
                sp.wait_ge(m_hi, count(i, w, 1, 1))
                sp.wait_ge(m_lo, count(i, w, 1, 1))
                for l in range(2):
                    sp.dma_start(QP[s][MROW + l:MROW + l + 1, :].bitcast(F32).rearrange("o (r q) -> o r q", q=P),
                                 mm[:, l, :].bitcast(F32)).then_inc(m_in[s], 16)

            store_xn(0)
            for hf in range(2):
                sp.wait_ge(xn_out[hf], 16)
            for b in range(2):
                rows(b, b, xst, xst_in)
            rows(0, 0, xa, xa_in)
            store_xn(1)
            sp.wait_ge(xt_ready, 1)
            rows(2, 0, xst, xst_in)
            store_xn(2)
            sp.wait_ge(pads_set, 2 * RING)
            store_qk(0, 0)
            pack(0, 0)
            store_qk(0, 1)
            store_xn(3)
            pack(0, 1)
            store_qk(0, 2)
            pack(0, 2)
            max_rows(0, 0)
            store_qk(0, 3)
            store_qk(0, 4)
            for hf in range(2):
                sp.wait_ge(xn_out[hf], 16 * (TT // GT))

            def step(i, w):
                m, b = w % 2, i * 2 + w // 2
                if exists(i, w, 3):
                    pack(i, w + 3)
                if m == 0 and exists(i, w, 6):
                    sp.wait_ge(xt_ready, b + 2)
                    rows(b + 3, (w // 2 + 1) % 2, xst, xst_in)
                if exists(i, w, 1):
                    max_rows(i, w + 1)
                if m == 0:
                    wait(sp, s_added, count(i, w, 1, 0))
                    if not (isinstance(i, int) and RING * i + w == 0):
                        store_s(b - 1)
                    if exists(i, w, 2):
                        rows(b + 1, (w // 2 + 1) % 2, xa, xa_in)
                if exists(i, w, AHEAD):
                    store_qk(i, w + AHEAD)

            def store_s(b):
                sp.dma_start(s_d[bass.ds(b * N, N), :].rearrange("(j p) c -> p j c", p=P), sst[:, :, :])\
                  .then_inc(s_out, 16)

            def body(i):
                for w in range(RING):
                    step(i, w)
            pairs(sp, body)
            for j in range(2):
                sp.wait_ge(scattered[j], 16 * B)
            sp.wait_ge(zero_out, 16 * PADS)

            def load_in(h, p, kind):
                row = q_of(h, p) * P if kind == "routed" else q_of(h, p) * P - FIRST_SHARED * P
                src = xs_d if kind == "routed" else xn_d
                sp.dma_start(xin[:, p, :], src[bass.ds(row, P), :]).then_inc(xin_in[p], 16)

            load_in(0, 0, "routed")
            load_in(0, 1, "routed")
            sp.wait_ge(s_added, UNITS)
            store_s(B - 1)
            sp.wait_ge(s_out, 16 * B)

            def turn(h, p, kind, last, nxt, after):
                q, (h1, p1) = q_of(h, p), before_turn(h, p)
                if after:
                    sp.wait_ge(xf_ready, q + 1)
                    load_in(h + 1, p, after)
                if isinstance(q, int) and q == 2:
                    for h, w in enumerate((wsg, wsu)):
                        sp.dma_start(SRAW[:, :, h * F:(h + 1) * F], w.rearrange("(k p) f -> p k f", p=P))\
                          .then_inc(sh_in, 16)
                    for h in range(2):
                        sp.dma_start(SRAW[:, h, 2 * F:].rearrange("p (k c) -> p k c", c=D),
                                     wsd[h * 2 * P:(h + 1) * 2 * P, :].rearrange("(k p) c -> p k c", p=P)).then_inc(sh_in, 16)
                if kind == "shared":
                    row = q * P - FIRST_SHARED * P
                    wait(sp, o_done, q - (FIRST_SHARED + 1))
                    sp.dma_start(sl[:, p, :], s_d[bass.ds(row, P), :]).then_inc(fin_in[p], 16)
                    sp.dma_start(xl[:, p, :], x[bass.ds(row, P), :]).then_inc(fin_in[p], 16)
                if last == "routed":
                    sp.wait_ge(y_copied, q)
                    sp.dma_start(ys_d[bass.ds(q * P - P, P), :], yb[:, p1, :]).then_inc(y_out[p1], 16)
                if last == "shared":
                    sp.wait_ge(o_done, q - FIRST_SHARED)
                    sp.dma_start(out[bass.ds(q * P - (1 + FIRST_SHARED) * P, P), :], ob[:, p1, :])\
                      .then_inc(o_out[p1], 16)
            turn.engine = sp
            turns(turn)
            for p in range(2):
                sp.wait_ge(o_out[p], 16 * TT // 2)

        @block.gpsimd
        def _(pool):
            g = nc.gpsimd
            g.memset(RW[:, :, :].rearrange("p k c -> p (k c)"), 0.0).then_inc(rw_set, 1)
            g.memset(zero[:, :], 0.0).then_inc(zero_set, 1)
            g.memset(ident[:, :], 0.0).then_inc(pool_const, 1)
            g.memset(before[:, :], 1.0).then_inc(pool_const, 1)
            g.memset(ones[:, :], 1.0).then_inc(pool_const, 1)
            g.iota(em8i[:, :, :], pattern=[[0, TT], [1, E]], base=-E, channel_multiplier=0).then_inc(pool_const, 1)
            g.iota(steps_i[:, :, :], pattern=[[0, E], [P, TT]], base=0, channel_multiplier=0).then_inc(pool_const, 1)
            g.iota(slot_i[:, :, :], pattern=[[1, SLOTS + 1], [0, E]], base=0, channel_multiplier=0)\
             .then_inc(pool_const, 1)
            g.iota(pad_i[:, :, :], pattern=[[P, PADS], [0, E]], base=0, channel_multiplier=1).then_inc(pool_const, 1)
            pool.wait_ge(pool_const, 7)
            g.affine_select(out=ident[:, :], in_=ident[:, :], compare_op=ALU.not_equal, fill=1.0, base=0,
                            pattern=[[-1, P]], channel_multiplier=1).then_inc(pool_const, 1)
            g.affine_select(out=before[:, :], in_=before[:, :], compare_op=ALU.is_gt, fill=0.0, base=0,
                            pattern=[[1, P]], channel_multiplier=-1).then_inc(pool_const, 1)
            g.memset(V[:, :, :, :, DH:].rearrange("p a b h c -> p (a b h) c"), 0.0)
            for w in range(RING):
                g.memset(QP[w][:, :].bitcast(F32), 0.0).then_inc(pads_set, 1)
                g.memset(KP[w][:, :].bitcast(F32), 0.0).then_inc(pads_set, 1)
                if w == 1:
                    pool.wait_ge(const_in, 16 * 6)
                    g.tensor_copy(W3HI[:, :, :, :], W3RAW[:, :, :, :]).then_inc(w3_hi, 1)
                    pool.wait_ge(w3_hi, 1)
                    g.tensor_tensor(W3LO[:, :, :, :], W3RAW[:, :, :, :], W3HI[:, :, :, :].bitcast(F32), ALU.subtract)\
                     .then_inc(w3_split, 1)
            pool.wait_ge(pads_set, 2 * RING)
            g.memset(V[:, :, :, :, DH:DH + 1].rearrange("p a b h c -> p (a b h) c"), 1.0).then_inc(pads_set, 1)
            pool.wait_ge(pads_set, 2 * RING + 1)
            for w in range(RING):
                g.memset(KP[w][MROW:MROW + 2, :].bitcast(F32), 1.0).then_inc(pads_set, 1)
            pool.wait_ge(pads_set, 3 * RING + 1)

            pool.wait_ge(zero_set, 1)
            pool.wait_ge(routed, 1)
            for hf in range(2):
                pool.wait_ge(xn_out[hf], 16 * (TT // GT))

            def fill_free_rows(i):
                wait(pool, zero_out, i * 16)
                g.tensor_copy(idx_pad[:, :], pad_row[:, bass.ds(i, 1)]).then_inc(pad_set, 1)
                pool.wait_ge(pad_set, i + 1)
                pool.sem_inc(fills_sent, 1)
                g.indirect_dma_start(out=xs_d, out_offset=bass.IndirectOffsetOnAxis(ap=idx_pad[:, :], axis=0),
                                     in_=zero[:, :], in_offset=None).then_inc(zero_out, 16)

            gu_halves = wgu.rearrange("e (k p) f -> (e k) p f", p=P)
            dn_halves = wdn.rearrange("e (h k p) c -> (e h) k p c", h=2, p=P)

            def load_half(n, slot, there):
                pool.dma_start(WRAW[:, bass.ds(slot, 1), 0:2 * F],
                               gu_halves[bass.ds(n, 1)].rearrange("o p f -> p (o f)")).then_inc(there, 16)
                pool.dma_start(WRAW[:, bass.ds(slot, 1), 2 * F:].rearrange("p o (k c) -> p (o k) c", c=D),
                               dn_halves[bass.ds(n, 1)].rearrange("o k p c -> p (o k) c")).then_inc(there, 16)

            def split(raw, hi, lo, n, done):
                g.tensor_copy(hi, raw).then_inc(hi_set, 1)
                pool.wait_ge(hi_set, n)
                pool.sem_inc(splits_begun, 1)
                g.tensor_tensor(lo, raw, hi.bitcast(F32), ALU.subtract).then_inc(done, 1)

            def split_part(slot, part, n):
                split(*(w[:, bass.ds(slot, 1), part * WH // 2:(part + 1) * WH // 2] for w in (WRAW, WHI, WLO)),
                      n, w_split)

            def scatter(i, w):
                b, par = i * 2 + w // 2, (w // 2) % 2
                pool.wait_ge(xa_in[par], i * 16 + 16)
                for j in range(2):
                    wait(pool, scattered[j], b * 16)
                    g.tensor_copy(idx2[:, j:j + 1], dest[:, bass.ds(b * 2 + j, 1)]).then_inc(xr_ready, 1)
                    g.tensor_tensor(xr[:, j, :], xa[:, par, j, :],
                                    score[:, bass.ds(b * 2 + j, 1)].to_broadcast([P, D]), ALU.mult).then_inc(xr_ready, 1)
                pool.wait_ge(xr_ready, b * 4 + 4)
                pool.sem_inc(batches_sent, 1)
                for j in range(2):
                    g.indirect_dma_start(out=xs_d, out_offset=bass.IndirectOffsetOnAxis(ap=idx2[:, j:j + 1], axis=0),
                                         in_=xr[:, j, :], in_offset=None).then_inc(scattered[j], 16)

            def add_xn(i, w):
                m, par = w % 2, (w // 2) % 2
                pool.wait_ge(normed, count(i, w, 1, 1))
                cols = slice(P * m, P * m + P)
                g.tensor_tensor(sst[:, :, cols], sst[:, :, cols], xa[:, par, :, cols], ALU.add).then_inc(s_added, 1)

            def body(i):
                for w in range(RING):
                    if w % 2 == 0:
                        scatter(i, w)
                    if not (isinstance(i, int) and i == 0 and w == 0):
                        add_xn(i, w - 1)
                    loads = not isinstance(i, int) or i < 2 * WRING
                    if w == 0 and loads:
                        s, use = slot_use(i, 1)
                        pool.wait_ge(m_in[s], use * 32)
                        load_half(i, i, half_in)
                    if w == 1 and loads:
                        pool.wait_ge(half_in, i * 32 + 32)
                    if w % 2 == 1 and loads:
                        split_part(i, w // 2, i * 2 + (w // 2 + 1))
                    if w == 3 and not (isinstance(i, int) and i == PADS):
                        fill_free_rows(i)
            pairs(pool, body)
            add_xn(PAIRS, -1)

            for first in range(WRING, E, WRING):
                with pool.Fori(0, min(WRING, E - first)) as e:
                    done = pool.value_load(slots_by[0:1, bass.ds(e + (first - WRING), 1)], min_val=1, max_val=SLOTS)
                    pool.wait_ge(y_ready, done)
                    for h in range(2):
                        load_half(e * 2 + (2 * first + h), e * 2 + h, late_in[h])
                    for h in range(2):
                        pool.wait_ge(late_in[h], e * 32 + (32 * (first - WRING) + 32))
                        for part in range(2):
                            split_part(e * 2 + h, part, e * SPLITS + (first * SPLITS + 2 * h + part + 1))
            pool.wait_ge(sh_in, 4 * 16)
            for h in range(2):
                split(SRAW[:, h, :], SHI[:, h, :], SLO[:, h, :], E * SPLITS + h + 1, sh_split)

            def turn(h, p, kind, last, nxt, after):
                q, (h1, p1) = q_of(h, p), before_turn(h, p)
                if kind == "shared":
                    if isinstance(q, int) and q == FIRST_SHARED:
                        for k in range(2):
                            pool.wait_ge(y_out[k], 16 * ((SLOTS + 1 - k) // 2))
                    pool.wait_ge(y_copied, q - 1)
                    g.tensor_copy(idx3[:, p:p + 1], dest[:, bass.ds(q - FIRST_SHARED, 1)]).then_inc(idx_set, 1)
                    pool.wait_ge(idx_set, q - (FIRST_SHARED - 1))
                    pool.sem_inc(tiles_fetched, 1)
                    g.indirect_dma_start(out=rb[:, p, :], out_offset=None, in_=ys_d,
                                         in_offset=bass.IndirectOffsetOnAxis(ap=idx3[:, p:p + 1], axis=0))\
                     .then_inc(r_in[p], 16)
                if last == "shared":
                    use = shared_use(h1, p1)
                    pool.wait_ge(z_silu, q - FIRST_SHARED)
                    pool.wait_ge(fin_in[p1], use * 32)
                    g.tensor_tensor(o1[:, p1, :], gz[:, p1, :], sl[:, p1, :], ALU.mult).then_inc(gated, 1)
                    pool.wait_ge(gated, q - FIRST_SHARED)
                    wait(pool, o_out[p1], use * 16 - 16)
                    g.tensor_tensor(ob[:, p1, :], o1[:, p1, :], xl[:, p1, :], ALU.add).then_inc(o_done, 1)
            turn.engine = pool
            turns(turn)

        @block.scalar
        def _(act):
            a_ = nc.scalar

            def roots(c):
                some = slice(c * GT, (c + 1) * GT)
                act.wait_ge(var_done, c + 1)
                a_.activation(root[:, some], var[:, some], ACT.Sqrt).then_inc(root_done, 1)

            def copy_t(i):
                def tile(j):
                    act.wait_ge(tr_ready, i * GT + j + 1)
                    if j % 4 == 0:
                        wait(act, lm_ready, i * 2 + (j // 4 - 1))
                    a_.activation(xT0[:, j // 4, :, j % 4 * P:(j % 4 + 1) * P],
                                  ps[:, j % 2, 0:N].rearrange("p (k c) -> p k c", k=KD), ACT.Copy).then_inc(tr_copied, 1)

                def group(n):
                    act.wait_ge(lm_ready, i * 2 + n + 1)
                    wait(act, lg_ready, i * 2 + (n - 1))
                    a_.activation(lT[:, n, :], ps[:, ST + n, 0:P], ACT.Copy).then_inc(lt_copied, 1)
                for j in range(GT - 1):
                    tile(j)
                group(0)
                tile(GT - 1)
                group(1)
            def xt_copy(b, par):
                act.wait_ge(xt_ready, b + 1)
                a_.activation(xT[:, par, 0, :, :].rearrange("p k c -> p (k c)"), ps[:, TRN, :], ACT.Copy)\
                  .then_inc(xt_hi, 1)

            def hi_parts(i, w):
                act.wait_ge(qk_ready, count(i, w, 1, 1))
                if not (isinstance(i, int) and RING * i + w == 0):
                    s, use = slot_use(i, w - 1) if w % RING else (RING - 1, i + w // RING)
                    act.wait_ge(qk_out[s], use * 16)
                for a in range(2):
                    ins = a_.activation(stag[:, a, 0, :], ps[:, PROJ, a * N:(a + 1) * N], ACT.Identity,
                                        bias=bqk[:, a, w % 2:w % 2 + 1])
                ins.then_inc(qk_hi, 1)

            def max_hi(i, w):
                act.wait_ge(mt_ready, count(i, w, 1, 1))
                if not (isinstance(i, int) and RING * i + w == 0):
                    s, use = slot_use(i, w - 1) if w % RING else (RING - 1, i + w // RING)
                    act.wait_ge(m_in[s], use * 32)
                a_.mul(mm[:, 0, :], ps[0:16, TRN, 0:P], -1.0).then_inc(m_hi, 1)

            roots(0)
            copy_t(0)
            roots(1)
            copy_t(1)
            roots(2)
            xt_copy(0, 0)
            act.wait_ge(const_in, 16 * 6)
            hi_parts(0, 0)
            xt_copy(1, 1)
            copy_t(2)
            roots(3)
            hi_parts(0, 1)
            copy_t(3)
            hi_parts(0, 2)
            act.wait_ge(neg_max, 1)
            a_.activation(score[:, :], tmp[:, :], ACT.Exp, scale=-1.0).then_inc(exp_max, 1)
            max_hi(0, 0)
            hi_parts(0, 3)
            xt_copy(2, 0)
            hi_parts(0, 4)

            def exps(i, w, c):
                gr, kt, hp = c // 4, c // 2 % 2, c % 2
                act.wait_ge(st_ready, count(i, w, 8, c + 1))
                if hp == 0:
                    wait(act, pv_done, count(i, w, 4, 2 * gr + kt - 1))
                a_.activation(PT[:, kt, hp * 512:hp * 512 + 512], ps[:, ST + c % 2, :], ACT.Exp,
                              scale=DH ** -0.5).then_inc(exp_done, 1)

            def o_copy(i, w, gr):
                act.wait_ge(pv_done, count(i, w, 4, 2 * gr + 2))
                wait(act, ot_ready, count(i, w, 1, 0))
                a_.activation(OTs[:, gr, :], ps[:, PV, 0:N], ACT.Copy).then_inc(o_copied, 1)

            def step(i, w):
                for c in range(5):
                    exps(i, w, c)
                if exists(i, w, 1):
                    max_hi(i, w + 1)
                exps(i, w, 5)
                o_copy(i, w, 0)
                if w % 2 == 1 and exists(i, w, AHEAD):
                    xt_copy(i * 2 + (w // 2 + 3), (w // 2 + 1) % 2)
                exps(i, w, 6)
                exps(i, w, 7)
                if exists(i, w, AHEAD):
                    hi_parts(i, w + AHEAD)
                o_copy(i, w, 1)

            def body(i):
                for w in range(RING):
                    step(i, w)
            pairs(act, body)

            def xf_round(h, p):
                q = q_of(h, p)
                act.wait_ge(xf_ready, q + 1)
                wait(act, up_ready, q - 1)
                a_.activation(xTf[:, p, 0, :], ps[:, 5, 0:D], ACT.Copy).then_inc(xf_hi, 1)
            xf_round(0, 0)

            def turn(h, p, kind, last, nxt, after):
                q, (h1, p1) = q_of(h, p), before_turn(h, p)
                if kind:
                    act.wait_ge(gate_ready, q + 1)
                    wait(act, h_done, q - 1)
                    a_.activation(sgb[:, p, :], ps[:, 2 * p, :], ACT.Silu).then_inc(silu_done, 1)
                if last:
                    act.wait_ge(ht_ready, q)
                    wait(act, y_ready, q - 2)
                    a_.activation(hTs[:, p1, 0, :], ps[:, 4, :], ACT.Copy).then_inc(ht_hi, 1)
                if nxt:
                    xf_round(*((h, 1) if p == 0 else (h + 1, 0)))
                if last == "shared":
                    act.wait_ge(y_copied, q)
                    a_.activation(gz[:, p1, :], yb[:, p1, :], ACT.Silu).then_inc(z_silu, 1)
            turn.engine = act
            turns(turn)

        @block.vector
        def _(dve):
            v = nc.vector
            done = [0]

            def chain(ins):
                done[0] += 1
                ins.then_inc(link, 1)
                dve.wait_ge(link, done[0])

            def take_logits(n):
                dve.wait_ge(lg_ready, n + 1)
                v.tensor_copy(lg[:, 4 * n:4 * n + 4, :],
                              ps[:, LT[n % 2], 0:4 * EC].rearrange("p (t c) -> p t c", c=EC)[:, :, 0:E])\
                 .then_inc(lg_copied, 1)

            def moments(c):
                some = slice(c * GT, (c + 1) * GT)
                dve.wait_ge(x_in[c], 16)
                for t in range(c * GT, (c + 1) * GT):
                    ins = v.bn_stats(stats[:, t, :], x_all[:, t, :])
                chain(ins)
                for t in range(c * GT, (c + 1) * GT):
                    ins = v.bn_aggr(mv[:, t, :], stats[:, t, :])
                chain(ins)
                v.tensor_scalar(var[:, some], mv[:, some, 1], EPS, None, ALU.add).then_inc(var_done, 1)
                dve.wait_ge(root_done, c + 1)
                chain(v.reciprocal(rstd[:, some], root[:, some]))
                chain(v.tensor_tensor(tmp[:, some], rstd[:, some], rstd[:, some], ALU.mult))
                chain(v.tensor_tensor(tmp[:, some], tmp[:, some], var[:, some], ALU.mult))
                chain(v.tensor_scalar(tmp[:, some], tmp[:, some], -0.5, 1.5, ALU.mult, ALU.add))
                chain(v.tensor_tensor(rstd[:, some], rstd[:, some], tmp[:, some], ALU.mult))

            def normalise(c):
                for j in range(GT):
                    t = c * GT + j
                    wait(dve, tr_ready, t - (GT - 1))
                    if j % (GT // 2) == 0:
                        wait(dve, xn_out[2 * j // GT], c * 16)
                    v.tensor_scalar(xnr[:, j, :], x_all[:, t, :], mv[:, t, 0:1], rstd[:, t:t + 1],
                                    ALU.subtract, ALU.mult).then_inc(xn_ready, 1)

            def route_top1():
                dve.wait_ge(lg_copied, TT // 4)
                chain(v.reduce_max(tmp[:, :], lg[:, :, :], AX.X))
                dve.sem_inc(neg_max, 1)
                chain(v.tensor_tensor(oh[:, :, :], lg[:, :, :], tmp[:, :].rearrange("p (t o) -> p t o", o=1)
                                      .to_broadcast([P, TT, E]), ALU.is_equal))
                chain(v.tensor_tensor(cand[:, :, :], oh[:, :, :], em8[:, :, :], ALU.mult))
                chain(v.tensor_reduce(mean[:, :], cand[:, :, :], AX.X, ALU.min))
                v.tensor_tensor(oh[:, :, :], em8[:, :, :], mean[:, :].rearrange("p (t o) -> p t o", o=1)
                                .to_broadcast([P, TT, E]), ALU.is_equal).then_inc(oh_ready, 1)

            def route_counts():
                dve.wait_ge(exp_max, 1)
                chain(v.tensor_scalar(score[:, :], score[:, :], 1.0, None, ALU.add))
                chain(v.reciprocal(score[:, :], score[:, :]))
                dve.wait_ge(rank_ready, 1)
                v.tensor_copy(rank[:, :, :].rearrange("p t e -> p (t e)"), ps[:, ST, 0:TT * E])
                chain(v.tensor_copy(cand[:, :, :].rearrange("p t e -> p (t e)"), ps[:, ST + 1, 0:TT * E]))
                dve.sem_inc(rank_read, 1)
                chain(v.memset(lg[:, :, 0], 1.0))
                for e in range(E):
                    ins = v.tensor_tensor_scan(incl[:, :, e], lg[:, :, 0], cand[:, :, e], 0.0, ALU.mult, ALU.add)
                chain(ins)

            def route_slots():
                chain(v.tensor_tensor(steps[:, :, :], incl[:, TT - 1, :].rearrange("p (e o) -> p e o", o=1)
                                      .to_broadcast([P, E, TT]), steps[:, :, :], ALU.is_gt))
                chain(v.reduce_sum(nt[:, :], steps[:, :, :], AX.X))
                chain(v.tensor_scalar(nt[:, :], nt[:, :], 1.0, None, ALU.max))
                chain(v.tensor_tensor_scan(tend[:, :], lg[:, 0:E, 0], nt[:, :], 0.0, ALU.mult, ALU.add))
                chain(v.tensor_tensor(base[:, :], tend[:, :], nt[:, :], ALU.subtract))
                chain(v.tensor_scalar(base[:, :], base[:, :], float(P), None, ALU.mult))
                chain(v.tensor_copy(cnt[:, :], incl[:, TT - 1, :]))

            def route_rows():
                chain(v.tensor_tensor(incl[:, :, :], incl[:, :, :], cand[:, :, :], ALU.subtract))
                chain(v.tensor_tensor(incl[:, :, :], incl[:, :, :], base[:, :].rearrange("p (o e) -> p o e", o=1)
                                      .to_broadcast([P, TT, E]), ALU.add))
                chain(v.tensor_tensor(incl[:, :, :].rearrange("p t e -> p (t e)"),
                                      incl[:, :, :].rearrange("p t e -> p (t e)"),
                                      rank[:, :, :].rearrange("p t e -> p (t e)"), ALU.add))
                chain(v.tensor_tensor(incl[:, :, :], incl[:, :, :], oh[:, :, :], ALU.mult))
                chain(v.reduce_sum(destf[:, :], incl[:, :, :], AX.X))
                chain(v.tensor_copy(dest[:, :], destf[:, :]))

            def route_tables():
                chain(v.tensor_tensor_scan(free[:, :], ones[:, 0:E], cnt[:, :], 0.0, ALU.mult, ALU.add))
                chain(v.tensor_scalar(base[:, :], tend[:, :], float(P), None, ALU.mult))
                chain(v.tensor_tensor(free[:, :], base[:, :], free[:, :], ALU.subtract))
                chain(v.tensor_tensor(pad_c[:, :, 1:E], pad_f[:, :, 1:E], free[:, 0:E - 1].rearrange("p (o e) -> p o e", o=1)
                                      .to_broadcast([P, PADS, E - 1]), ALU.is_ge))
                chain(v.memset(pad_c[:, :, 0], 1.0))
                chain(v.tensor_tensor(pad_c[:, :, :], pad_c[:, :, :], cnt[:, :].rearrange("p (o e) -> p o e", o=1)
                                      .to_broadcast([P, PADS, E]), ALU.mult))
                chain(v.reduce_sum(pad_s[:, :], pad_c[:, :, :], AX.X))
                chain(v.tensor_tensor(pad_s[:, :], pad_s[:, :], pad_f[:, :, 0], ALU.add))
                v.tensor_copy(pad_row[:, :], pad_s[:, :])
                chain(v.tensor_tensor(slot_f[:, :, :], slot_f[:, :, :], tend[:, :].rearrange("p (o e) -> p o e", o=1)
                                      .to_broadcast([P, SLOTS + 1, E]), ALU.is_ge))
                chain(v.reduce_sum(eidf[:, :], slot_f[:, :, :], AX.X))
                chain(v.tensor_scalar(eidf[:, :], eidf[:, :], float(E - 1), None, ALU.min))
                chain(v.tensor_copy(sel[:, :], eidf[:, :]))
                for e in range(WRING, E, WRING):
                    chain(v.tensor_scalar(cntf[:, :], eidf[:, :], float(e), float(-WRING), ALU.is_ge, ALU.mult))
                    chain(v.tensor_tensor(sel[:, :], sel[:, :], cntf[:, :], ALU.add))
                chain(v.tensor_scalar(sel[:, :], sel[:, :], 2.0, None, ALU.mult))
                v.tensor_copy(half_at[0:1, :], sel[0:1, :])
                chain(v.tensor_scalar(cntf[:, :], eidf[:, :], float(SPLITS), float(SPLITS), ALU.mult, ALU.add))
                v.tensor_copy(splits_by[0:1, :], cntf[0:1, :])
                v.tensor_copy(slots_by[0:1, :], tend[0:1, :]).then_inc(routed, 1)

            def lo_parts(i, w):
                dve.wait_ge(qk_hi, count(i, w, 1, 1))
                for a in range(2):
                    ins = v.scalar_tensor_tensor(stag[:, a, 1, :], ps[:, PROJ, a * N:(a + 1) * N],
                                                 bqk[:, a, w % 2:w % 2 + 1], stag[:, a, 0, :].bitcast(F32),
                                                 ALU.add, ALU.subtract)
                ins.then_inc(qk_lo, 1)

            def xt_rest(b, par):
                dve.wait_ge(xt_hi, b + 1)
                v.tensor_tensor(xT[:, par, 1, :, :].rearrange("p k c -> p (k c)"), ps[:, TRN, :],
                                xT[:, par, 0, :, :].rearrange("p k c -> p (k c)").bitcast(F32), ALU.subtract)\
                 .then_inc(xt_lo, 1)

            def v_copy(n_done, par, j):
                dve.wait_ge(v_ready, n_done)
                v.tensor_tensor(V[:, par, j, :, 0:DH], ps[:, PROJ, 0:D].rearrange("p (h d) -> p h d", d=DH),
                                bvb[:, :].rearrange("p (h d) -> p h d", d=DH), ALU.add).then_inc(v_copied, 1)

            def reduce_chunk(i, w, c):
                j, hp = c // 4, c % 4
                dve.wait_ge(s_ready, count(i, w, SC, c + 1))
                v.reduce_max(mx[:, w % 2, 2 * hp:2 * hp + 2, j], SA[c % 3], AX.X).then_inc(s_reduced, 1)

            def max_lo(i, w):
                dve.wait_ge(m_hi, count(i, w, 1, 1))
                v.scalar_tensor_tensor(mm[:, 1, :], ps[0:16, TRN, 0:P], -1.0, mm[:, 0, :].bitcast(F32),
                                       ALU.mult, ALU.subtract).then_inc(m_lo, 1)

            def norm(i, w):
                dve.wait_ge(ot_ready, count(i, w, 1, 1))
                o = ps[:, TRN, :].rearrange("p (g j h c) -> p g j h c", g=2, j=2, h=4)
                v.reciprocal(rden[:, :], ps[:, TRN, :].rearrange("p (r c) -> p r c", c=2 * DH)[:, :, DH])\
                 .then_inc(inv_done, 1)
                dve.wait_ge(inv_done, count(i, w, 1, 1))
                if w % 2 == 0:
                    wait(dve, s_out, (i * 2 + w // 2) * 16)
                inv = rden[:, :].rearrange("p (g j h o) -> p g j h o", g=2, j=2, h=4)
                for gr in range(2):
                    col = P * (w % 2) + 4 * DH * gr
                    ins = v.tensor_tensor(sst[:, :, col:col + 4 * DH].rearrange("p j (h d) -> p j h d", d=DH),
                                          o[:, gr, :, :, 0:DH], inv[:, gr, :, :, :].to_broadcast([P, 2, 4, DH]), ALU.mult)
                ins.then_inc(normed, 1)

            for c in range(3):
                moments(c)
                if c == 2:
                    xt_rest(0, 0)
                normalise(c)
                if c > 0:
                    take_logits(2 * c - 2)
                    take_logits(2 * c - 1)
            dve.wait_ge(const_in, 16 * 6)
            lo_parts(0, 0)
            xt_rest(1, 1)
            moments(3)
            lo_parts(0, 1)
            normalise(3)
            take_logits(4)
            take_logits(5)
            dve.wait_ge(pool_const, 9)
            v.tensor_copy(em8[:, :, :], em8i[:, :, :])
            v.tensor_copy(steps[:, :, :], steps_i[:, :, :])
            v.tensor_copy(slot_f[:, :, :], slot_i[:, :, :])
            v.tensor_copy(pad_f[:, :, :], pad_i[:, :, :])
            take_logits(6)
            take_logits(7)
            lo_parts(0, 2)
            route_top1()
            dve.wait_ge(pads_set, 3 * RING + 1)
            v_copy(1, 0, 0)
            for c in range(SC):
                if c == SC // 2:
                    v_copy(2, 0, 1)
                reduce_chunk(0, 0, c)
            max_lo(0, 0)
            route_counts()
            lo_parts(0, 3)
            xt_rest(2, 0)
            route_slots()
            route_rows()
            lo_parts(0, 4)
            for c in range(SC):
                reduce_chunk(0, 1, c)
            route_tables()

            def step(i, w):
                first = isinstance(i, int) and RING * i + w == 0

                def ahead(c):
                    if exists(i, w, 2):
                        reduce_chunk(i, w + 2, c)
                ahead(0)
                if not first:
                    norm(i, w - 1)
                ahead(1)
                ahead(2)
                ahead(3)
                if exists(i, w, 1):
                    max_lo(i, w + 1)
                ahead(4)
                ahead(5)
                if exists(i, w, 2):
                    v_copy(count(i, w, 1, 3), (w // 2 + 1) % 2, w % 2)
                if w % 2 == 1 and exists(i, w, AHEAD):
                    xt_rest(i * 2 + (w // 2 + 3), (w // 2 + 1) % 2)
                ahead(6)
                ahead(7)
                if exists(i, w, AHEAD):
                    lo_parts(i, w + AHEAD)

            def body(i):
                for w in range(RING):
                    step(i, w)
            pairs(dve, body)
            norm(PAIRS, -1)

            def xf_rest(h, p):
                dve.wait_ge(xf_hi, q_of(h, p) + 1)
                v.tensor_tensor(xTf[:, p, 1, :], ps[:, 5, 0:D], xTf[:, p, 0, :].bitcast(F32), ALU.subtract)\
                 .then_inc(xf_lo, 1)
            xf_rest(0, 0)

            def turn(h, p, kind, last, nxt, after):
                q, (h1, p1) = q_of(h, p), before_turn(h, p)
                if last:
                    dve.wait_ge(ht_hi, q)
                    v.tensor_tensor(hTs[:, p1, 1, :], ps[:, 4, :], hTs[:, p1, 0, :].bitcast(F32), ALU.subtract)\
                     .then_inc(ht_lo, 1)
                if kind:
                    dve.wait_ge(silu_done, q + 1)
                    dve.wait_ge(up_ready, q + 1)
                    wait(dve, ht_ready, q - 1)
                    v.tensor_tensor(hb[:, p, :], sgb[:, p, :], ps[:, 2 * p + 1, :], ALU.mult).then_inc(h_done, 1)
                if nxt:
                    xf_rest(*((h, 1) if p == 0 else (h + 1, 0)))
                if last:
                    dve.wait_ge(y_ready, q)
                    y = ps[:, 6 + p1, 0:D]
                    if last == "routed":
                        wait(dve, y_out[p1], h1 * 16)
                        v.tensor_copy(yb[:, p1, :], y).then_inc(y_copied, 1)
                    else:
                        if isinstance(q, int) and q <= FIRST_SHARED + 2:
                            for k in range(2):
                                dve.wait_ge(y_out[k], 16 * ((SLOTS + 1 - k) // 2))
                        wait(dve, z_silu, q - (FIRST_SHARED + 2))
                        dve.wait_ge(r_in[p1], shared_use(h1, p1) * 16)
                        v.tensor_tensor(yb[:, p1, :], y, rb[:, p1, :], ALU.add).then_inc(y_copied, 1)
            turn.engine = dve
            turns(turn)

        @block.tensor
        def _(pe):
            mmul = nc.tensor.matmul
            pe.wait_ge(pool_const, 9)
            pe.wait_ge(rw_in, 16)

            def transpose(dst, src):
                return nc.tensor.transpose(dst, src, ident[:, :])

            def logits(i):
                def tr(j):
                    pe.wait_ge(xn_ready, i * GT + j + 1)
                    wait(pe, tr_copied, i * GT + j - 1)
                    for k in range(KD):
                        ins = transpose(ps[:, j % 2, k * P:(k + 1) * P], xnr[:, j, k * P:(k + 1) * P])
                    ins.then_inc(tr_ready, 1)

                def group(n):
                    pe.wait_ge(tr_copied, i * GT + 4 * n + 4)
                    wait(pe, lt_copied, i * 2 + (n - 1))
                    for k in range(KD):
                        for t in range(4):
                            ins = mmul(ps[EC * t:EC * t + EC, ST + n, 0:P], RW[:, k, :], xT0[:, n, k, t * P:(t + 1) * P],
                                       start=(k == 0), stop=(k == KD - 1), tile_position=(0, EC * t))
                    ins.then_inc(lm_ready, 1)

                def by_token(n):
                    pe.wait_ge(lt_copied, i * 2 + n + 1)
                    wait(pe, lg_copied, i * 2 + (n - 1))
                    transpose(ps[:, LT[n], 0:P], lT[:, n, :]).then_inc(lg_ready, 1)
                for j in range(6):
                    tr(j)
                group(0)
                tr(6)
                tr(7)
                by_token(0)
                group(1)
                by_token(1)

            def xt(b, par, nth):
                pe.wait_ge(xst_in[par], nth * 16)
                for j in range(2):
                    for k in range(KD):
                        ins = transpose(ps[:, TRN, k * N + j * P:k * N + (j + 1) * P],
                                        xst[:, par, j, k * P:(k + 1) * P])
                ins.then_inc(xt_ready, 1)

            def qk(w, par):
                for a in range(2):
                    for n, (wp, xp) in enumerate(TERMS):
                        for k in range(KD):
                            ins = mmul(ps[:, PROJ, a * N:(a + 1) * N], W3[wp][:, a, k, w % 2 * P:(w % 2 + 1) * P],
                                       xT[:, par, xp, k, :], start=(n == 0 and k == 0), stop=(n == 2 and k == KD - 1))
                ins.then_inc(qk_ready, 1)

            def v_tile(par, j):
                for n, (xp, wp) in enumerate(TERMS):
                    for k in range(KD):
                        ins = mmul(ps[:, PROJ, 0:D], xT[:, par, xp, k, j * P:(j + 1) * P], W3[wp][:, 2, k, :],
                                   start=(n == 0 and k == 0), stop=(n == 2 and k == KD - 1))
                ins.then_inc(v_ready, 1)

            def scores(i, w, c):
                s, use = slot_use(i, w)
                j, hp = c // 4, c % 4
                if c == 0:
                    pe.wait_ge(packed[s], use * 64)
                wait(pe, s_reduced, count(i, w, SC, (-1, 0, -2)[c] if c < 3 else c - 2))
                for h in range(2):
                    col = (2 * hp + h) * N
                    ins = mmul(SA[c % 3][:, h, :], QP[s][0:SPLIT_ROWS, col + j * P:col + (j + 1) * P],
                               KP[s][0:SPLIT_ROWS, col:col + N], start=True, stop=True)
                ins.then_inc(s_ready, 1)

            def max_t(i, w):
                pe.wait_ge(s_reduced, count(i, w, SC, SC))
                transpose(ps[0:16, TRN, 0:P], mx[:, w % 2, :, :].rearrange("p h j -> p (h j)")).then_inc(mt_ready, 1)

            def scores_t(i, w, c):
                s, use = slot_use(i, w)
                gr, kt, hp = c // 4, c // 2 % 2, c % 2
                if c == 0:
                    pe.wait_ge(m_in[s], use * 32)
                wait(pe, exp_done, count(i, w, 8, c - 1))
                for h in range(2):
                    col = (4 * gr + 2 * hp + h) * N
                    ins = mmul(ps[:, ST + c % 2, h * N:(h + 1) * N], KP[s][:, col + kt * P:col + (kt + 1) * P],
                               QP[s][:, col:col + N], start=True, stop=True)
                ins.then_inc(st_ready, 1)

            def weighted(i, w, gr, kt):
                pe.wait_ge(exp_done, count(i, w, 8, 4 * gr + 2 * kt + 2))
                if kt == 0:
                    wait(pe, o_copied, count(i, w, 2, gr))
                for h in range(4):
                    head = UH * (w % 2) + 4 * gr + h
                    ins = mmul(ps[32 * h:32 * h + 32, PV, 0:N], V[:, (w // 2) % 2, kt, head, :],
                               PT[:, kt, h * N:(h + 1) * N], start=(kt == 0), stop=(kt == 1),
                               tile_position=(0, 32 * h))
                ins.then_inc(pv_done, 1)

            def out_t(i, w):
                pe.wait_ge(o_copied, count(i, w, 2, 2))
                for gr in range(2):
                    for j in range(2):
                        c = (2 * gr + j) * P
                        ins = transpose(ps[:, TRN, c:c + P], OTs[:, gr, j * P:(j + 1) * P])
                ins.then_inc(ot_ready, 1)

            logits(0)
            logits(1)
            xt(0, 0, 1)
            pe.wait_ge(w3_split, 1)
            pe.wait_ge(xt_lo, 1)
            qk(0, 0)
            xt(1, 1, 1)
            logits(2)
            pe.wait_ge(qk_lo, 1)
            qk(1, 0)
            logits(3)
            pe.wait_ge(qk_lo, 2)
            pe.wait_ge(xt_lo, 2)
            qk(2, 1)
            pe.wait_ge(lg_copied, TT // 4)
            pe.wait_ge(qk_lo, 3)
            v_tile(0, 0)
            for c in range(3):
                scores(0, 0, c)
            pe.wait_ge(oh_ready, 1)
            hot = oh[:, :, :].rearrange("p t e -> p (t e)")
            mmul(ps[:, ST, 0:TT * E], before[:, :], hot, start=True, stop=True)
            mmul(ps[:, ST + 1, 0:TT * E], ones[:, :], hot, start=True, stop=True).then_inc(rank_ready, 1)
            pe.wait_ge(v_copied, 1)
            v_tile(0, 1)
            for c in range(3, SC):
                scores(0, 0, c)
            max_t(0, 0)
            pe.wait_ge(v_copied, 2)
            qk(3, 1)
            pe.wait_ge(m_lo, 1)
            xt(2, 0, 2)
            pe.wait_ge(xt_lo, 3)
            pe.wait_ge(qk_lo, 4)
            qk(4, 0)
            for c in range(SC):
                scores(0, 1, c)
            pe.wait_ge(rank_read, 1)

            def step(i, w):
                m, par = w % 2, w // 2
                first = isinstance(i, int) and RING * i + w == 0

                def ahead(c):
                    if exists(i, w, 2):
                        scores(i, w + 2, c)
                scores_t(i, w, 0)
                ahead(0)
                scores_t(i, w, 1)
                ahead(1)
                if not first:
                    pe.wait_ge(m_lo, count(i, w, 1, 1))
                    out_t(i, w - 1)
                scores_t(i, w, 2)
                ahead(2)
                scores_t(i, w, 3)
                weighted(i, w, 0, 0)
                ahead(3)
                scores_t(i, w, 4)
                if exists(i, w, 1):
                    if not first:
                        pe.wait_ge(normed, count(i, w, 1, 0))
                    max_t(i, w + 1)
                ahead(4)
                scores_t(i, w, 5)
                weighted(i, w, 0, 1)
                ahead(5)
                if exists(i, w, 2):
                    if exists(i, w, AHEAD - 1):
                        pe.wait_ge(qk_lo, count(i, w, 1, AHEAD))
                    else:
                        pe.wait_ge(v_copied, count(i, w, 1, 2))
                    v_tile(1 - par, m)
                if m == 1 and exists(i, w, AHEAD):
                    pe.wait_ge(m_lo, count(i, w, 1, 2))
                    xt(None, 1 - par, i + 2 + par)
                scores_t(i, w, 6)
                ahead(6)
                scores_t(i, w, 7)
                weighted(i, w, 1, 0)
                ahead(7)
                if exists(i, w, AHEAD):
                    pe.wait_ge(v_copied, count(i, w, 1, 3))
                    if m == 1:
                        pe.wait_ge(xt_lo, i * 2 + (par + 4))
                    qk(w + AHEAD, par if m == 0 else 1 - par)
                weighted(i, w, 1, 1)

            def body(i):
                for w in range(RING):
                    step(i, w)
            pairs(pe, body)

            def xf(h, p):
                q = q_of(h, p)
                pe.wait_ge(xin_in[p], h * 16 + 16)
                wait(pe, xf_lo, q)
                for k in range(KD):
                    ins = transpose(ps[:, 5, k * P:(k + 1) * P], xin[:, p, k * P:(k + 1) * P])
                ins.then_inc(xf_ready, 1)

            pe.wait_ge(exp_done, 8 * UNITS)
            xf(0, 0)
            pe.wait_ge(normed, UNITS - 1)
            out_t(PAIRS, -1)
            pe.wait_ge(w_split, WRING * SPLITS)
            pe.wait_ge(s_reduced, SC * UNITS)

            here_reg, was_reg, next_reg = (nc.alloc_registers(name, engines=[mybir.EngineType.PE])
                                           for name in ("here", "was", "next"))
            for reg in (here_reg, was_reg):
                nc.regs_load(reg, half_at[0:1, 0:1])

            def turn(h, p, kind, last, nxt, after):
                q, (h1, p1) = q_of(h, p), before_turn(h, p)

                def product(bank, width, xT, chunks, weights, at, hi_there, lo_there):
                    for n, (xp, wp) in enumerate(TERMS):
                        if n == 0:
                            pe.wait_ge(hi_there, at)
                        if n == 2:
                            pe.wait_ge(lo_there, at)
                        for k in range(chunks):
                            ins = mmul(ps[:, bank, 0:width], xT[:, xp, k * P:(k + 1) * P], weights(wp, k),
                                       start=(n == 0 and k == 0), stop=(n == 2 and k == chunks - 1))
                    return ins

                def gate_up(half):
                    def weights(part, k):
                        cols = slice(half * F, (half + 1) * F)
                        if kind == "shared":
                            return (SHI, SLO)[part][:, k, cols]
                        return (WHI, WLO)[part][:, bass.ds(here + k, 1), cols]
                    return product(2 * p + half, F, xTf[:, p, :, :], KD, weights, q + 1, xf_hi, xf_lo)

                def down():
                    def weights(part, k):
                        cols = slice(2 * F + k % 2 * D, 2 * F + (k % 2 + 1) * D)
                        if last == "shared":
                            return (SHI, SLO)[part][:, k // 2, cols]
                        return (WHI, WLO)[part][:, bass.ds(was + k // 2, 1), cols]
                    return product(6 + p1, D, hTs[:, p1, :, :], KF, weights, q, ht_hi, ht_lo)
                if kind == "shared" and isinstance(q, int) and q == FIRST_SHARED:
                    pe.wait_ge(sh_split, 2)
                here, was = (nc.snap(reg, min_val=0, max_val=2 * WRING - 2) for reg in (here_reg, was_reg))
                if kind:
                    wait(pe, silu_done, q - 1)
                    gate_up(0).then_inc(gate_ready, 1)
                if last:
                    pe.wait_ge(h_done, q)
                    wait(pe, ht_lo, q - 1)
                    for k in range(KF):
                        ins = transpose(ps[:, 4, k * P:(k + 1) * P], hb[:, p1, k * P:(k + 1) * P])
                    ins.then_inc(ht_ready, 1)
                if kind:
                    wait(pe, h_done, q - 1)
                    gate_up(1).then_inc(up_ready, 1)
                if nxt:
                    xf(*((h, 1) if p == 0 else (h + 1, 0)))
                if nxt == "routed":
                    splits = pe.value_load(splits_by[0:1, bass.ds(q + 1, 1)], min_val=SPLITS, max_val=SPLITS * E)
                    nc.regs_load(next_reg, half_at[0:1, bass.ds(q + 1, 1)])
                    pe.wait_ge(w_split, splits)
                if isinstance(q, int) and q == 2:
                    pe.wait_ge(normed, UNITS)
                if last:
                    wait(pe, y_copied, q - 2)
                    down().then_inc(y_ready, 1)
                if kind == "routed":
                    nc.regs_mov(was_reg, here)
                if nxt == "routed":
                    nc.regs_mov(here_reg, nc.snap(next_reg, min_val=0, max_val=2 * WRING - 2))
            turn.engine = pe
            turns(turn)


def kernel(**inputs):
    import numpy as np
    import concourse.bacc as bacc
    from concourse.bass_utils import run_bass_kernel_spmd

    a = {k[3:]: np.asarray(v) for k, v in inputs.items()}

    def by_dim(w):
        return np.ascontiguousarray(w.reshape(w.shape[:-1] + (2, UH, DH)).swapaxes(-1, -2).reshape(w.shape))

    arrays = {
        "x": a["attn_x"].reshape(T, D),
        "wq": by_dim(a["attn_Wq"]), "wk": by_dim(a["attn_Wk"]), "wv": a["attn_Wv"],
        "bq": by_dim(a["attn_bq"]).reshape(2, P).T, "bk": by_dim(a["attn_bk"]).reshape(2, P).T,
        "bv": a["attn_bv"].reshape(1, D), "rw": a["ffn_router_w"].T,
        "wgu": a["ffn_gate_up_proj"], "wdn": a["ffn_down_proj"],
        "wsg": a["ffn_shared_gate_w"], "wsu": a["ffn_shared_up_w"], "wsd": a["ffn_shared_down_w"],
    }
    nc = bacc.Bacc("TRN2", target_bir_lowering=False, num_devices=1)
    maps, args = {}, []
    for name, v in arrays.items():
        v = np.ascontiguousarray(v)
        maps["in_" + name] = v
        args.append(nc.dram_tensor("in_" + name, v.shape, F32, kind="ExternalInput").ap())
    args.append(nc.dram_tensor("out", (T, D), F32, kind="ExternalOutput").ap())
    build(nc, *args)
    r = run_bass_kernel_spmd(nc, [maps], core_ids=[0])
    return r.results[0]["out"].reshape(B, N, D)
```
